# Optimizing a Trainium2 kernel written in Bass

```python
import numpy as np
import jax
import jax.numpy as jnp

def _softmax(x, axis=-1):
    return jax.nn.softmax(x, axis=axis)

def _gelu(x):
    return jax.nn.gelu(x, approximate=True)

def _silu(x):
    return jax.nn.silu(x)

def _sigmoid(x):
    return jax.nn.sigmoid(x)

def _layernorm(x, axis=-1, eps=1e-05):
    m = jnp.mean(x, axis=axis, keepdims=True)
    v = jnp.var(x, axis=axis, keepdims=True)
    return (x - m) / jnp.sqrt(v + eps)

def _scatter_add(tgt, idx, src, axis=0):
    return tgt.at[idx].add(src)

def _segment_sum(src, seg, n):
    return jax.ops.segment_sum(src, seg, n)
kernel_name = 'mk_gnn_preln_d2_gnn_r8_1e7563'

def setup_inputs(seed: int=0):
    np.random.seed(seed)
    _w = jnp.asarray

    def _rec_inputs():
        import jax
        import jax.numpy as jnp
        _gk = jax.random.key(seed)
        x = -0.000202 + 1 * jax.random.normal(jax.random.fold_in(_gk, 1), (12500, 64), jnp.float32)
        src = jax.random.randint(jax.random.fold_in(_gk, 2), (200000,), 0, 12500, jnp.int32)
        dst = jnp.minimum((12500 * jax.random.uniform(jax.random.fold_in(_gk, 3), (200000,)) ** 2.0).astype(jnp.int32), 99999)
        _o = jnp.argsort(dst, stable=True)
        src = src[_o]
        dst = dst[_o]
        edge_attr_50 = jax.random.uniform(jax.random.fold_in(_gk, 12), (200000, 50), jnp.float32, 0.0, 1)
        return (x, src, dst, edge_attr_50)
    x, src, dst, edge_attr_50 = _rec_inputs()

    def _L0_gnn_setup():
        import jax, jax.numpy as jnp
        import numpy as np
        N = 12500
        E = 200000
        D_IN, D_H, D_OUT = (64, 64, 64)

        def _gcn_conv(x, W, b, src, dst, norm):
            h = x @ W
            msg = h[src] * norm[:, None]
            out = jax.ops.segment_sum(msg, dst, num_segments=N)
            return out + b
        key = jax.random.key(seed)
        ks = jax.random.split(key, 8)
        node_embed = jax.random.normal(ks[0], (N, D_IN), dtype=jnp.float32)
        message_edge = jax.random.randint(ks[1], (2, E), 0, N, dtype=jnp.int32)
        s = 0.05
        W1 = jax.random.normal(ks[2], (D_IN, D_H), dtype=jnp.float32) * s
        b1 = jnp.zeros((D_H,), dtype=jnp.float32)
        W2 = jax.random.normal(ks[3], (D_H, D_H), dtype=jnp.float32) * s
        b2 = jnp.zeros((D_H,), dtype=jnp.float32)
        W3 = jax.random.normal(ks[4], (D_H, D_OUT), dtype=jnp.float32) * s
        b3 = jnp.zeros((D_OUT,), dtype=jnp.float32)
        return {'node_embed': node_embed, 'message_edge': message_edge, 'W1': W1, 'b1': b1, 'W2': W2, 'b2': b2, 'W3': W3, 'b3': b3}
    _L0_gnn_all = _L0_gnn_setup()
    _L0_gnn_in = {k: v for k, v in _L0_gnn_all.items() if k in ('W1', 'b1', 'W2', 'b2', 'W3', 'b3')}
    del _L0_gnn_all

    def _L1_gnn_setup():
        import jax, jax.numpy as jnp
        import numpy as np
        N_NODES = 12500
        N_EDGES = 200000
        D_IN = 64
        D_RADIAL = 50
        D_HIDDEN = 64
        D_OUT = 64
        key = jax.random.key(seed)
        ks = jax.random.split(key, 10)
        x = jax.random.normal(ks[0], (N_NODES, D_IN), dtype=jnp.float32)
        edge_basis = jax.random.uniform(ks[1], (N_EDGES, D_RADIAL), dtype=jnp.float32)
        src = jax.random.randint(ks[2], (N_EDGES,), 0, N_NODES, dtype=jnp.int32)
        dst = jax.random.randint(ks[3], (N_EDGES,), 0, N_NODES, dtype=jnp.int32)

        def lin(k, fan_in, fan_out):
            k1, k2 = jax.random.split(k)
            bound = 1.0 / np.sqrt(fan_in)
            W = jax.random.uniform(k1, (fan_out, fan_in), minval=-bound, maxval=bound, dtype=jnp.float32)
            b = jax.random.uniform(k2, (fan_out,), minval=-bound, maxval=bound, dtype=jnp.float32)
            return (W, b)
        W_pre, b_pre = lin(ks[4], D_IN, D_HIDDEN)
        W_rad, b_rad = lin(ks[5], D_RADIAL, D_HIDDEN)
        W_post, b_post = lin(ks[6], D_HIDDEN, D_OUT)
        return {'x': x, 'edge_basis': edge_basis, 'src': src, 'dst': dst, 'W_pre': W_pre, 'b_pre': b_pre, 'W_rad': W_rad, 'b_rad': b_rad, 'W_post': W_post, 'b_post': b_post}
    _L1_gnn_all = _L1_gnn_setup()
    _L1_gnn_in = {k: v for k, v in _L1_gnn_all.items() if k in ('W_pre', 'b_pre', 'W_rad', 'b_rad', 'W_post', 'b_post')}
    del _L1_gnn_all
    return {'x': x, 'src': src, 'dst': dst, 'edge_attr_50': edge_attr_50, 'L0_gnn_W1': _L0_gnn_in['W1'], 'L0_gnn_b1': _L0_gnn_in['b1'], 'L0_gnn_W2': _L0_gnn_in['W2'], 'L0_gnn_b2': _L0_gnn_in['b2'], 'L0_gnn_W3': _L0_gnn_in['W3'], 'L0_gnn_b3': _L0_gnn_in['b3'], 'L1_gnn_W_pre': _L1_gnn_in['W_pre'], 'L1_gnn_b_pre': _L1_gnn_in['b_pre'], 'L1_gnn_W_rad': _L1_gnn_in['W_rad'], 'L1_gnn_b_rad': _L1_gnn_in['b_rad'], 'L1_gnn_W_post': _L1_gnn_in['W_post'], 'L1_gnn_b_post': _L1_gnn_in['b_post']}

def reference(x, src, dst, edge_attr_50, L0_gnn_W1, L0_gnn_b1, L0_gnn_W2, L0_gnn_b2, L0_gnn_W3, L0_gnn_b3, L1_gnn_W_pre, L1_gnn_b_pre, L1_gnn_W_rad, L1_gnn_b_rad, L1_gnn_W_post, L1_gnn_b_post):
    import jax
    import jax.numpy as jnp

    def _L0_gnn_ref(node_embed, message_edge, W1, b1, W2, b2, W3, b3):
        import jax, jax.numpy as jnp
        import numpy as np
        N = 12500
        E = 200000
        D_IN, D_H, D_OUT = (64, 64, 64)

        def _gcn_conv(x, W, b, src, dst, norm):
            h = x @ W
            msg = h[src] * norm[:, None]
            out = jax.ops.segment_sum(msg, dst, num_segments=N)
            return out + b
        loop = jnp.arange(N, dtype=message_edge.dtype)
        src = jnp.concatenate([message_edge[0], loop])
        dst = jnp.concatenate([message_edge[1], loop])
        deg = jax.ops.segment_sum(jnp.ones_like(dst, dtype=jnp.float32), dst, num_segments=N)
        dinv = jnp.where(deg > 0, jax.lax.rsqrt(deg), 0.0)
        norm = dinv[src] * dinv[dst]
        x = jax.nn.relu(_gcn_conv(node_embed, W1, b1, src, dst, norm))
        x = jax.nn.relu(_gcn_conv(x, W2, b2, src, dst, norm))
        return _gcn_conv(x, W3, b3, src, dst, norm)

    def _L1_gnn_ref(x, edge_basis, src, dst, W_pre, b_pre, W_rad, b_rad, W_post, b_post):
        import jax, jax.numpy as jnp
        import numpy as np
        N_NODES = 12500
        N_EDGES = 200000
        D_IN = 64
        D_RADIAL = 50
        D_HIDDEN = 64
        D_OUT = 64
        hv = x @ W_pre.T + b_pre
        filt = edge_basis @ W_rad.T + b_rad
        msg = hv[src] * filt
        h = jax.ops.segment_sum(msg, dst, num_segments=N_NODES)
        return jax.nn.silu(h @ W_post.T + b_post)
    edge_index = jnp.stack([src, dst])
    h = jnp.maximum(_layernorm(x, axis=-1), 0.0)
    x = x + _L0_gnn_ref(h, edge_index, L0_gnn_W1, L0_gnn_b1, L0_gnn_W2, L0_gnn_b2, L0_gnn_W3, L0_gnn_b3)
    h = jnp.maximum(_layernorm(x, axis=-1), 0.0)
    x = x + _L1_gnn_ref(h, edge_attr_50, src, dst, L1_gnn_W_pre, L1_gnn_b_pre, L1_gnn_W_rad, L1_gnn_b_rad, L1_gnn_W_post, L1_gnn_b_post)
    return x

_drawn_inputs = setup_inputs


def setup_inputs(seed=0):
    import zlib

    import numpy as np

    out = dict(_drawn_inputs(seed))
    spreads = {'L0_gnn_b1': (0.0, 0.8), 'L0_gnn_b2': (0.0, 0.298), 'L0_gnn_b3': (0.0, 0.1)}
    factors = {'L0_gnn_W1': 3.163, 'L0_gnn_W2': 3.169}
    for name, (base, spread) in spreads.items():
        noise = np.random.default_rng([zlib.crc32(name.encode()), seed]).standard_normal(out[name].shape)
        drawn = base * np.exp(spread * noise) if base else spread * noise
        out[name] = jnp.asarray(drawn.astype(out[name].dtype))
    for name, factor in factors.items():
        out[name] = (out[name] * factor).astype(out[name].dtype)
    return out
```

```python
from contextlib import ExitStack

import concourse.bass as bass
import numpy as np
from concourse import mybir

F32 = mybir.dt.float32
BF16 = mybir.dt.bfloat16
I32 = mybir.dt.int32
ALU = mybir.AluOpType
ACT = mybir.ActivationFunctionType
AX = mybir.AxisListType

P = 128
NODES, EDGES, D, RADIAL = 12500, 200000, 64, 50
WINDOWS = -(-NODES // P)
LAST = NODES - (WINDOWS - 1) * P
PAD_NODES = WINDOWS * P
BLOCK_TILES = 8
BLOCK = BLOCK_TILES * P
BLOCKS = -(-EDGES // BLOCK)
TILES = BLOCKS * BLOCK_TILES
SLOTS = 4
ROUNDS = BLOCKS // SLOTS
GROUP = 7
GROUPS = WINDOWS // GROUP
GCN_LAYERS = 3
PASSES = GCN_LAYERS + 1
EPS = 1e-5
assert BLOCKS % SLOTS == 0 and WINDOWS % GROUP == 0 and GROUPS % 2 == 0


def gnn_program(nc, x, src, dst, radial, W1, b1, W2, b2, W3, b3, W_pre, b_pre, W_rad, b_rad, W_post, b_post, out):
    ctx = ExitStack()
    with ctx:
        def sbuf(name, shape, dt=F32):
            return ctx.enter_context(nc.sbuf_tensor(name, shape, dt))

        def psum(name, shape):
            return ctx.enter_context(nc.psum_tensor(name, shape, F32))

        def sem(name):
            return ctx.enter_context(nc.semaphore(name))

        table = nc.dram_tensor("table", (PAD_NODES, D), F32, kind="Internal").ap()
        table_pw = table.rearrange("(p w) f -> p w f", w=WINDOWS)

        src_i = sbuf("src_i", [P, TILES], I32)
        dst_i = sbuf("dst_i", [P, TILES], I32)
        row_i = sbuf("row_i", [P, TILES], I32)
        dst_f = sbuf("dst_f", [P, TILES])
        row_stage = sbuf("row_stage", [P, SLOTS * BLOCK_TILES], I32)
        rows = sbuf("rows", [P, SLOTS, BLOCK_TILES * D])
        onehot = sbuf("onehot", [P, BLOCK_TILES, P])
        onehot16 = sbuf("onehot16", [P, BLOCK_TILES, P], BF16)
        dst_rel = sbuf("dst_rel", [P, BLOCK_TILES])
        msg = sbuf("msg", [P, BLOCK_TILES * D])
        radial_sb = sbuf("radial_sb", [RADIAL + 1, SLOTS, BLOCK])
        xs = sbuf("xs", [P, WINDOWS, D])
        node = sbuf("node", [P, WINDOWS, D])
        sumT = sbuf("sumT", [D, PAD_NODES])
        square = sbuf("square", [P, WINDOWS, D])
        stage_nf = sbuf("stage_nf", [P, GROUP, D])
        stage_fn = sbuf("stage_fn", [D, 2, GROUP * P])
        tmp = sbuf("tmp", [P, GROUP, D])
        iota_i = sbuf("iota_i", [P, P], I32)
        iota = sbuf("iota", [P, P], BF16)
        ident = sbuf("ident", [P, P])
        wbase_i = sbuf("wbase_i", [P, WINDOWS], I32)
        wbase = sbuf("wbase", [P, WINDOWS])
        ones16 = sbuf("ones16", [P, 1], BF16)
        range_p = sbuf("range_p", [P, 2 * BLOCKS])
        range_p1 = sbuf("range_p1", [P, 2 * BLOCKS])
        span_f = sbuf("span_f", [1, 2 * BLOCKS])
        span_i = sbuf("span_i", [1, 2 * BLOCKS], I32)
        span = sbuf("span", [1, 2 * BLOCKS], I32)
        deg = sbuf("deg", [P, WINDOWS])
        root = sbuf("root", [P, WINDOWS])
        dinv = sbuf("dinv", [P, WINDOWS])
        mean = sbuf("mean", [P, WINDOWS])
        var = sbuf("var", [P, WINDOWS])
        std = sbuf("std", [P, WINDOWS])
        rstd = sbuf("rstd", [P, WINDOWS])
        w_gcn = [sbuf(f"w_gcn{i}", [D, D]) for i in range(GCN_LAYERS)]
        w_pre = sbuf("w_pre", [D, D])
        w_rad = sbuf("w_rad", [RADIAL + 1, D])
        w_post = sbuf("w_post", [D, D])
        bias = sbuf("bias", [P, 5, D])

        ps_sum = psum("ps_sum", [P, 512])
        ps_filt = psum("ps_filt", [P, 2, 512])
        ps_z = psum("ps_z", [P, 2, 512])
        ps_t = psum("ps_t", [P, 1024])

        loaded = sem("loaded")
        radial_loaded = [sem(f"radial_loaded{j}") for j in range(SLOTS)]
        gathered = [sem(f"gathered{j}") for j in range(SLOTS)]
        gather_turn = sem("gather_turn")
        flip_turn = sem("flip_turn")
        consts_made = sem("consts_made")
        row_ready = sem("row_ready")
        block_range = sem("block_range")
        range_all = sem("range_all")
        spans_ready = sem("spans_ready")
        step = sem("step")
        rows_staged = sem("rows_staged")
        slot_free = sem("slot_free")
        rel_ready = sem("rel_ready")
        onehot_ready = sem("onehot_ready")
        window_summed = sem("window_summed")
        filter_ready = sem("filter_ready")
        msg_ready = sem("msg_ready")
        root_wanted = sem("root_wanted")
        root_ready = sem("root_ready")
        sums_done = sem("sums_done")
        fn_staged = sem("fn_staged")
        z_ready = sem("z_ready")
        y_done = sem("y_done")
        nf_staged = sem("nf_staged")
        flipped = sem("flipped")
        flip_copied = sem("flip_copied")
        normed = sem("normed")
        table_written = sem("table_written")
        y_ready = sem("y_ready")
        exp_ready = sem("exp_ready")
        out_written = sem("out_written")

        N_LOADS = 4 + 5 + 5 + 2
        TRANSFORMS = 5
        PRE, POST = 3, 4

        def groups(g, n=1):
            return bass.ds(g * GROUP, GROUP)

        def nodes(g):
            return bass.ds(g * (GROUP * P), GROUP * P)

        def over_features(column):
            return column.unsqueeze(2).to_broadcast((P, column.shape[1], D))

        def over_windows(row, n):
            return row.unsqueeze(1).to_broadcast((P, n, D))

        block = ctx.enter_context(nc.Block())

        @block.sync
        def _(sp):
            sp.dma_start(src_i[:, :], src).then_inc(loaded, 16)
            sp.dma_start(dst_i[:, :], dst).then_inc(loaded, 16)
            sp.dma_start(xs[:, 0:WINDOWS - 1, :],
                         x[0:(WINDOWS - 1) * P, :].rearrange("(w p) f -> p w f", p=P)).then_inc(loaded, 16)
            sp.wait_ge(consts_made, 7)
            sp.dma_start(xs[0:LAST, WINDOWS - 1, :], x[(WINDOWS - 1) * P:NODES, :]).then_inc(loaded, 16)
            for w_sb, w in zip(w_gcn + [w_pre, w_post], (W1, W2, W3, W_pre, W_post)):
                sp.dma_start(w_sb[:, :], w).then_inc(loaded, 16)
            for i, b in enumerate((b1, b2, b3, b_pre, b_post)):
                sp.dma_start(bias[:, i, :], b.to_broadcast((P, D))).then_inc(loaded, 16)
            sp.dma_start(w_rad[0:RADIAL, :], W_rad).then_inc(loaded, 16)
            sp.dma_start(w_rad[RADIAL:RADIAL + 1, :], b_rad).then_inc(loaded, 16)
            for j in range(SLOTS):
                sp.dma_start(radial_sb[0:RADIAL, j, :],
                             radial[:, j * BLOCK:(j + 1) * BLOCK]).then_inc(radial_loaded[j], 16)

            for stage in (0, 1, 2, PRE + 1):
                with sp.Fori(0, GROUPS) as g:
                    sp.wait_ge(y_done, g + (stage * GROUPS + 1))
                    sp.dma_start(table_pw[:, groups(g), :], node[:, groups(g), :]).then_inc(table_written, 16)

            with sp.Fori(1, ROUNDS) as r:
                for j in range(SLOTS):
                    sp.wait_ge(filter_ready, r * SLOTS + (j + 1 - SLOTS))
                    sp.dma_start(radial_sb[0:RADIAL, j, :],
                                 radial[:, bass.ds(r * (SLOTS * BLOCK) + j * BLOCK, BLOCK)]
                                 ).then_inc(radial_loaded[j], 16)

            with sp.Fori(0, GROUPS - 1) as g:
                sp.wait_ge(y_done, g + ((POST + 1) * GROUPS + 1))
                sp.dma_start(out[nodes(g), :].rearrange("(w p) f -> p w f", p=P),
                             node[:, groups(g), :]).then_inc(out_written, 16)
            sp.wait_ge(y_done, (POST + 2) * GROUPS)
            first = (GROUPS - 1) * GROUP
            sp.dma_start(out[first * P:(WINDOWS - 1) * P, :].rearrange("(w p) f -> p w f", p=P),
                         node[:, first:WINDOWS - 1, :]).then_inc(out_written, 16)
            sp.dma_start(out[(WINDOWS - 1) * P:NODES, :], node[0:LAST, WINDOWS - 1, :]).then_inc(out_written, 16)
            sp.wait_ge(out_written, 16 * (GROUPS + 1))

        @block.gpsimd
        def _(pool):
            nc.gpsimd.memset(xs[:, WINDOWS - 1, :], 0.0).then_inc(consts_made, 1)
            nc.gpsimd.memset(radial_sb[:, :, :], 1.0).then_inc(consts_made, 1)
            nc.gpsimd.memset(ident[:, :], 0.0).then_inc(consts_made, 1)
            nc.gpsimd.memset(ones16[:, :], 1.0).then_inc(consts_made, 1)
            nc.gpsimd.iota(iota_i[:, :], pattern=[[1, P]], base=0, channel_multiplier=0).then_inc(consts_made, 1)
            nc.gpsimd.iota(wbase_i[:, :], pattern=[[P, WINDOWS]], base=0, channel_multiplier=0).then_inc(consts_made, 1)
            pool.wait_ge(consts_made, 6)
            nc.gpsimd.affine_select(out=ident[:, :], in_=ident[:, :], compare_op=ALU.not_equal, fill=1.0,
                                    base=0, pattern=[[-1, P]], channel_multiplier=1).then_inc(consts_made, 1)
            pool.wait_ge(block_range, 2)
            nc.gpsimd.partition_all_reduce(range_p1[:, :], range_p[:, :], P,
                                           bass.bass_isa.ReduceOp.max).then_inc(range_all, 1)

            def gather(p, j):
                pool.sem_inc(gather_turn, 1)
                for k in range(BLOCK_TILES):
                    c = j * BLOCK_TILES + k
                    nc.gpsimd.indirect_dma_start(
                        out=rows[:, j, k * D:(k + 1) * D], out_offset=None, in_=table[:, :],
                        in_offset=bass.IndirectOffsetOnAxis(ap=row_stage[:, c:c + 1], axis=0),
                    ).then_inc(gathered[j], 16)

            for p in range(PASSES):
                pool.wait_ge(table_written, 16 * GROUPS * (p + 1))
                for j in range(SLOTS):
                    pool.wait_ge(rows_staged, p * BLOCKS + j + 1)
                    gather(p, j)
                with pool.Fori(1, ROUNDS) as r:
                    for j in range(SLOTS):
                        pool.wait_ge(rows_staged, r * SLOTS + (p * BLOCKS + j + 1))
                        pool.wait_ge(slot_free, r * SLOTS + (p * BLOCKS + j + 1 - SLOTS))
                        gather(p, j)

        @block.scalar
        def _(act):
            def square_root(n, to, of):
                act.wait_ge(root_wanted, n + 1)
                nc.scalar.activation(to, of, ACT.Sqrt).then_inc(root_ready, 1)

            def flip(f):
                with act.Fori(0, GROUPS) as g:
                    nc.scalar.copy(stage_nf[:, :, :], node[:, groups(g), :]).then_inc(nf_staged, 1)
                    act.wait_ge(flipped, g + (f * GROUPS + 1))
                    nc.scalar.copy(sumT[:, nodes(g)], ps_t[0:D, 0:GROUP * P]).then_inc(flip_copied, 1)

            def transform(k):
                for h in range(2):
                    if k:
                        act.wait_ge(z_ready, k * GROUPS + h - 1)
                    stage_sums(h, h)
                with act.Fori(1, GROUPS // 2) as g:
                    for h in range(2):
                        act.wait_ge(z_ready, g * 2 + (k * GROUPS + h - 1))
                        stage_sums(h, g * 2 + h)

            def stage_sums(h, g):
                nc.scalar.copy(stage_fn[:, h, :], sumT[:, nodes(g)]).then_inc(fn_staged, 1)

            def stage_rows(r, j):
                nc.scalar.copy(row_stage[:, j * BLOCK_TILES:(j + 1) * BLOCK_TILES],
                               row_i[:, bass.ds(r * (SLOTS * BLOCK_TILES) + j * BLOCK_TILES, BLOCK_TILES)]
                               ).then_inc(rows_staged, 1)

            square_root(0, std[:, :], var[:, :])
            square_root(1, root[:, :], deg[:, :])
            act.wait_ge(row_ready, 1)
            for p in range(PASSES):
                for j in range(SLOTS):
                    if p:
                        act.wait_ge(gathered[j], 16 * BLOCK_TILES * ROUNDS * p)
                    stage_rows(0, j)
                if p < GCN_LAYERS:
                    act.wait_ge(y_done, (p + 1) * GROUPS)
                    flip(p)
                with act.Fori(1, ROUNDS) as r:
                    for j in range(SLOTS):
                        act.wait_ge(gathered[j], r * (16 * BLOCK_TILES) + 16 * BLOCK_TILES * ROUNDS * p)
                        stage_rows(r, j)
                act.wait_ge(sums_done, p + 1)
                if p < GCN_LAYERS:
                    transform(p)
                if p == GCN_LAYERS - 1:
                    square_root(2, std[:, :], var[:, :])
                    act.wait_ge(normed, 1)
                    flip(GCN_LAYERS)
                    act.wait_ge(flip_copied, (GCN_LAYERS + 1) * GROUPS)
                    transform(PRE)
            with act.Fori(0, GROUPS // 2) as g:
                for h in range(2):
                    act.wait_ge(z_ready, g * 2 + (POST * GROUPS + h - 1))
                    stage_sums(h, g * 2 + h)
                    act.wait_ge(y_ready, g * 2 + (h + 1))
                    nc.scalar.activation(tmp[:, :, :], tmp[:, :, :], ACT.Exp,
                                         scale=-1.0).then_inc(exp_ready, 1)

        @block.vector
        def _(dve):
            steps = [0]

            def then(ins):
                ins.then_inc(step, 1)
                steps[0] += 1

            def settle():
                dve.wait_ge(step, steps[0])

            def layernorm(n):
                then(nc.vector.tensor_reduce(mean[:, :], xs[:, :, :], AX.X, ALU.add))
                settle()
                then(nc.vector.tensor_scalar(mean[:, :], mean[:, :], 1.0 / D, None, ALU.mult))
                settle()
                then(nc.vector.tensor_tensor(node[:, :, :], xs[:, :, :], over_features(mean[:, :]), ALU.subtract))
                settle()
                then(nc.vector.tensor_tensor(square[:, :, :], node[:, :, :], node[:, :, :], ALU.mult))
                settle()
                then(nc.vector.tensor_reduce(var[:, :], square[:, :, :], AX.X, ALU.add))
                settle()
                nc.vector.tensor_scalar(var[:, :], var[:, :], 1.0 / D, EPS, ALU.mult, ALU.add).then_inc(root_wanted, 1)
                dve.wait_ge(root_ready, n)
                then(nc.vector.reciprocal(rstd[:, :], std[:, :]))
                settle()

            def one_hot_pair(to, r, j, w):
                nc.vector.tensor_scalar(dst_rel[:, :],
                                        dst_f[:, bass.ds(r * (SLOTS * BLOCK_TILES) + j * BLOCK_TILES, BLOCK_TILES)],
                                        wbase[:, bass.ds(w, 1)], None, ALU.subtract).then_inc(rel_ready, 1)
                dve.wait_ge(rel_ready, dve.snap(pair))
                for k in range(BLOCK_TILES):
                    one = nc.vector.tensor_scalar(to[:, k, :], iota[:, :], dst_rel[:, k:k + 1], None, ALU.is_equal)
                one.then_inc(onehot_ready, 1)
                dve.wait_ge(window_summed, dve.snap(pair))
                dve.reg_add(pair, pair, 1)

            def block_span(r, j):
                b = r * (2 * SLOTS) + 2 * j
                lo = dve.value_load(span[0:1, bass.ds(b, 1)], min_val=0, max_val=WINDOWS - 1)
                hi = dve.value_load(span[0:1, bass.ds(b + 1, 1)], min_val=1, max_val=WINDOWS)
                return lo, hi

            dve.wait_ge(loaded, 16 * N_LOADS)
            dve.wait_ge(consts_made, 7)
            then(nc.vector.tensor_copy(dst_f[:, :], dst_i[:, :]))
            then(nc.vector.tensor_copy(iota[:, :], iota_i[:, :]))
            then(nc.vector.tensor_copy(wbase[:, :], wbase_i[:, :]))
            settle()
            by_block = dst_f[:, :].rearrange("p (b k) -> p b k", k=BLOCK_TILES)
            nc.vector.tensor_reduce(range_p[:, 0:BLOCKS], by_block, AX.X, ALU.min, negate=True).then_inc(block_range, 1)
            nc.vector.tensor_reduce(range_p[:, BLOCKS:], by_block, AX.X, ALU.max).then_inc(block_range, 1)
            then(nc.vector.tensor_single_scalar(row_i[:, :], src_i[:, :], P - 1, ALU.bitwise_and))
            then(nc.vector.tensor_single_scalar(dst_i[:, :], src_i[:, :], 7, ALU.logical_shift_right))
            settle()
            nc.vector.scalar_tensor_tensor(row_i[:, :], row_i[:, :], float(WINDOWS), dst_i[:, :],
                                           ALU.mult, ALU.add).then_inc(row_ready, 1)
            then(nc.vector.memset(deg[:, :], 1.0))
            dve.wait_ge(range_all, 1)
            then(nc.vector.tensor_scalar(span_f[:, 0:BLOCKS], range_p1[0:1, 0:BLOCKS], -1.0, None, ALU.mult))
            then(nc.vector.tensor_copy(span_f[:, BLOCKS:], range_p1[0:1, BLOCKS:]))
            settle()
            then(nc.vector.tensor_copy(span_i[:, :], span_f[:, :]))
            settle()
            then(nc.vector.tensor_single_scalar(span_i[:, :], span_i[:, :], 7, ALU.logical_shift_right))
            settle()
            then(nc.vector.tensor_copy(span_f[:, :], span_i[:, :]))
            settle()
            by_two = span[:, :].rearrange("p (b two) -> p two b", two=2)
            nc.vector.tensor_copy(by_two[:, 0, :], span_f[:, 0:BLOCKS]).then_inc(spans_ready, 1)
            nc.vector.tensor_scalar(by_two[:, 1, :], span_f[:, BLOCKS:], 1.0, None, ALU.add).then_inc(spans_ready, 1)
            layernorm(1)
            then(nc.vector.tensor_tensor(node[:, :, :], node[:, :, :], over_features(rstd[:, :]), ALU.mult))
            settle()

            dve.wait_ge(spans_ready, 2)
            pair = dve.alloc_register("dve_pair")
            dve.reg_mov(pair, 1)
            with dve.Fori(0, ROUNDS) as r:
                for j in range(SLOTS):
                    lo, hi = block_span(r, j)
                    with dve.Fori(lo, hi) as w:
                        one_hot_pair(onehot16, r, j, w)
                        nc.vector.tensor_tensor(deg[:, bass.ds(w, 1)], deg[:, bass.ds(w, 1)], ps_sum[:, 0:1], ALU.add)
            then(nc.vector.memset(tmp[:, :, :], 0.0))
            settle()
            dve.nop().then_inc(root_wanted, 1)
            dve.wait_ge(root_ready, 2)
            then(nc.vector.reciprocal(dinv[:, :], root[:, :]))
            settle()
            with dve.Fori(0, GROUPS) as g:
                nc.vector.scalar_tensor_tensor(node[:, groups(g), :], node[:, groups(g), :], 0.0,
                                               over_features(dinv[:, groups(g)]), ALU.max, ALU.mult).then_inc(y_done, 1)

            for p in range(PASSES):
                if p < GCN_LAYERS:
                    dve.wait_ge(flip_copied, (p + 1) * GROUPS)
                else:
                    then(nc.vector.memset(sumT[:, :], 0.0))
                    settle()
                with dve.Fori(0, ROUNDS) as r:
                    for j in range(SLOTS):
                        if p == GCN_LAYERS:
                            dve.wait_ge(filter_ready, r * SLOTS + (j + 1))
                            dve.wait_ge(gathered[j], r * (16 * BLOCK_TILES) + 16 * BLOCK_TILES * (ROUNDS * p + 1))
                            nc.vector.tensor_tensor(msg[:, :], rows[:, j, :], ps_filt[:, j % 2, :],
                                                    ALU.mult).then_inc(msg_ready, 1)
                        lo, hi = block_span(r, j)
                        with dve.Fori(lo, hi) as w:
                            one_hot_pair(onehot, r, j, w)
                            nc.vector.tensor_tensor(sumT[:, bass.ds(w * P, P)], sumT[:, bass.ds(w * P, P)],
                                                    ps_sum[0:D, 0:P], ALU.add)
                        dve.nop().then_inc(slot_free, 1)
                dve.drain().then_inc(sums_done, 1)

                k = p if p < GCN_LAYERS else POST
                at = steps[0]
                with dve.Fori(0, GROUPS // 2) as g2:
                    for h in range(2):
                        g = g2 * 2 + h
                        z = ps_z[:, h, 0:GROUP * D].rearrange("p (w f) -> p w f", f=D)
                        dve.wait_ge(z_ready, g2 * 2 + (k * GROUPS + h + 1))
                        norm = over_features(dinv[:, groups(g)])
                        b = over_windows(bias[:, k, :], GROUP)
                        if k == POST:
                            nc.vector.tensor_tensor(node[:, groups(g), :], z, b, ALU.add).then_inc(step, 1)
                            dve.wait_ge(y_done, g2 * 2 + ((k + 1) * GROUPS + h))
                            dve.wait_ge(step, g2 * 8 + (at + 4 * h + 1))
                            nc.vector.tensor_scalar(tmp[:, :, :], node[:, groups(g), :], -87.0, None,
                                                    ALU.max).then_inc(y_ready, 1)
                            dve.wait_ge(exp_ready, g2 * 2 + (h + 1))
                            nc.vector.tensor_scalar(tmp[:, :, :], tmp[:, :, :], 1.0, None, ALU.add).then_inc(step, 1)
                            dve.wait_ge(step, g2 * 8 + (at + 4 * h + 2))
                            nc.vector.reciprocal(tmp[:, :, :], tmp[:, :, :]).then_inc(step, 1)
                            dve.wait_ge(step, g2 * 8 + (at + 4 * h + 3))
                            nc.vector.tensor_tensor(tmp[:, :, :], node[:, groups(g), :], tmp[:, :, :],
                                                    ALU.mult).then_inc(step, 1)
                            dve.wait_ge(step, g2 * 8 + (at + 4 * h + 4))
                            nc.vector.tensor_tensor(node[:, groups(g), :], tmp[:, :, :], xs[:, groups(g), :],
                                                    ALU.add).then_inc(y_done, 1)
                            continue
                        dve.wait_ge(y_done, g2 * 2 + ((k + 1) * GROUPS + h))
                        nc.vector.tensor_tensor(tmp[:, :, :], z, norm, ALU.mult).then_inc(step, 1)
                        dve.wait_ge(step, g2 * 4 + (at + 2 * h + 1))
                        nc.vector.tensor_tensor(tmp[:, :, :], tmp[:, :, :], b, ALU.add).then_inc(step, 1)
                        dve.wait_ge(step, g2 * 4 + (at + 2 * h + 2))
                        if k < GCN_LAYERS - 1:
                            nc.vector.scalar_tensor_tensor(node[:, groups(g), :], tmp[:, :, :], 0.0, norm,
                                                           ALU.max, ALU.mult).then_inc(y_done, 1)
                        else:
                            nc.vector.tensor_tensor(xs[:, groups(g), :], xs[:, groups(g), :], tmp[:, :, :],
                                                    ALU.add).then_inc(y_done, 1)
                steps[0] += (4 if k == POST else 2) * GROUPS
                if p == GCN_LAYERS - 1:
                    dve.wait_ge(y_done, (p + 2) * GROUPS)
                    layernorm(3)
                    then(nc.vector.tensor_tensor(node[:, :, :], node[:, :, :], over_features(rstd[:, :]), ALU.mult))
                    settle()
                    nc.vector.tensor_scalar(node[:, :, :], node[:, :, :], 0.0, None, ALU.max).then_inc(normed, 1)
                    dve.wait_ge(flip_copied, (GCN_LAYERS + 1) * GROUPS)
                    with dve.Fori(0, GROUPS // 2) as g2:
                        for h in range(2):
                            z = ps_z[:, h, 0:GROUP * D].rearrange("p (w f) -> p w f", f=D)
                            dve.wait_ge(z_ready, g2 * 2 + (PRE * GROUPS + h + 1))
                            nc.vector.tensor_tensor(node[:, groups(g2 * 2 + h), :], z,
                                                    over_windows(bias[:, PRE, :], GROUP), ALU.add).then_inc(y_done, 1)

        @block.tensor
        def _(pe):
            pe.wait_ge(loaded, 16 * N_LOADS)
            pe.wait_ge(consts_made, 7)
            pe.wait_ge(spans_ready, 2)
            pair = pe.alloc_register("pe_pair")
            pe.reg_mov(pair, 1)

            def block_span(r, j):
                b = r * (2 * SLOTS) + 2 * j
                lo = pe.value_load(span[0:1, bass.ds(b, 1)], min_val=0, max_val=WINDOWS - 1)
                hi = pe.value_load(span[0:1, bass.ds(b + 1, 1)], min_val=1, max_val=WINDOWS)
                return lo, hi

            def flip(f):
                with pe.Fori(0, GROUPS) as g:
                    pe.wait_ge(nf_staged, g + (f * GROUPS + 1))
                    pe.sem_inc(flip_turn, 1)
                    for i in range(GROUP):
                        t = nc.tensor.transpose(ps_t[0:D, i * P:(i + 1) * P], stage_nf[:, i, :], ident[:, :])
                    t.then_inc(flipped, 1)

            def transform(k, w):
                with pe.Fori(0, GROUPS // 2) as g:
                    for h in range(2):
                        pe.wait_ge(fn_staged, g * 2 + (k * GROUPS + h + 1))
                        pe.wait_ge(y_done, g * 2 + ((k + 1) * GROUPS + h - 1))
                        for i in range(GROUP):
                            z = nc.tensor.matmul(ps_z[:, h, i * D:(i + 1) * D], stage_fn[:, h, i * P:(i + 1) * P],
                                                 w[:, :], start=True, stop=True)
                        z.then_inc(z_ready, 1)

            with pe.Fori(0, ROUNDS) as r:
                for j in range(SLOTS):
                    lo, hi = block_span(r, j)
                    with pe.Fori(lo, hi):
                        pe.wait_ge(onehot_ready, pe.snap(pair))
                        for k in range(BLOCK_TILES):
                            s = nc.tensor.matmul(ps_sum[:, 0:1], onehot16[:, k, :], ones16[:, :],
                                                 start=(k == 0), stop=(k == BLOCK_TILES - 1))
                        s.then_inc(window_summed, 1)
                        pe.reg_add(pair, pair, 1)

            for p in range(PASSES):
                if p < GCN_LAYERS:
                    flip(p)
                with pe.Fori(0, ROUNDS) as r:
                    for j in range(SLOTS):
                        if p == GCN_LAYERS:
                            pe.wait_ge(radial_loaded[j], r * 16 + 16)
                            for k in range(BLOCK_TILES):
                                f = nc.tensor.matmul(ps_filt[:, j % 2, k * D:(k + 1) * D],
                                                     radial_sb[:, j, k * P:(k + 1) * P], w_rad[:, :],
                                                     start=True, stop=True)
                            f.then_inc(filter_ready, 1)
                            pe.wait_ge(msg_ready, r * SLOTS + (j + 1))
                        else:
                            pe.wait_ge(gathered[j], r * (16 * BLOCK_TILES) + 16 * BLOCK_TILES * (ROUNDS * p + 1))
                        lo, hi = block_span(r, j)
                        with pe.Fori(lo, hi):
                            pe.wait_ge(onehot_ready, pe.snap(pair))
                            for k in range(BLOCK_TILES):
                                of = (msg[:, k * D:(k + 1) * D] if p == GCN_LAYERS
                                      else rows[:, j, k * D:(k + 1) * D])
                                s = nc.tensor.matmul(ps_sum[0:D, 0:P], of, onehot[:, k, :],
                                                     start=(k == 0), stop=(k == BLOCK_TILES - 1))
                            s.then_inc(window_summed, 1)
                            pe.reg_add(pair, pair, 1)
                if p < GCN_LAYERS:
                    transform(p, w_gcn[p])
                if p == GCN_LAYERS - 1:
                    flip(GCN_LAYERS)
                    transform(PRE, w_pre)
            transform(POST, w_post)


def kernel(x, src, dst, edge_attr_50, L0_gnn_W1, L0_gnn_b1, L0_gnn_W2, L0_gnn_b2, L0_gnn_W3, L0_gnn_b3,
           L1_gnn_W_pre, L1_gnn_b_pre, L1_gnn_W_rad, L1_gnn_b_rad, L1_gnn_W_post, L1_gnn_b_post):
    import concourse.bacc as bacc
    from concourse.bass_utils import run_bass_kernel_spmd

    def by_tile(a, fill):
        a = np.concatenate([np.asarray(a), np.full(BLOCKS * BLOCK - EDGES, fill, np.int32)])
        return np.ascontiguousarray(a.reshape(TILES, P).T)

    def row(b):
        return np.ascontiguousarray(np.asarray(b).reshape(1, -1))

    def turned(w):
        return np.ascontiguousarray(np.asarray(w).T)

    radial = np.zeros((RADIAL, BLOCKS * BLOCK), np.float32)
    radial[:, :EDGES] = np.asarray(edge_attr_50).T
    arrays = {
        "x": np.ascontiguousarray(x),
        "src": by_tile(src, 0),
        "dst": by_tile(dst, NODES),
        "radial": radial,
        "W1": np.ascontiguousarray(L0_gnn_W1), "b1": row(L0_gnn_b1),
        "W2": np.ascontiguousarray(L0_gnn_W2), "b2": row(L0_gnn_b2),
        "W3": np.ascontiguousarray(L0_gnn_W3), "b3": row(L0_gnn_b3),
        "W_pre": turned(L1_gnn_W_pre), "b_pre": row(L1_gnn_b_pre),
        "W_rad": turned(L1_gnn_W_rad), "b_rad": row(L1_gnn_b_rad),
        "W_post": turned(L1_gnn_W_post), "b_post": row(L1_gnn_b_post),
    }
    nc = bacc.Bacc("TRN2", target_bir_lowering=False, num_devices=1)
    args = {name: nc.dram_tensor(f"in_{name}", a.shape, mybir.dt.from_np(a.dtype), kind="ExternalInput").ap()
            for name, a in arrays.items()}
    out = nc.dram_tensor("out", (NODES, D), F32, kind="ExternalOutput").ap()
    gnn_program(nc, out=out, **args)
    result = run_bass_kernel_spmd(nc, [{f"in_{name}": a for name, a in arrays.items()}], core_ids=[0])
    return result.results[0]["out"]
```

```python
from contextlib import ExitStack

import concourse.bass as bass
import numpy as np
from concourse import mybir

F32 = mybir.dt.float32
BF16 = mybir.dt.bfloat16
F16 = mybir.dt.float16
F8 = mybir.dt.float8e4
I32 = mybir.dt.int32
ALU = mybir.AluOpType
ACT = mybir.ActivationFunctionType
AX = mybir.AxisListType
REDUCE = bass.bass_isa.ReduceOp

P = 128
NODES, EDGES, D, RADIAL = 12500, 200000, 64, 50
WINDOWS = -(-NODES // P)
LAST = NODES - (WINDOWS - 1) * P
PAD_NODES = WINDOWS * P
SPAN = 160
MORE = 128
SUMS = PAD_NODES + SPAN
BLOCK_TILES = 8
BLOCK = BLOCK_TILES * P
BLOCKS = -(-EDGES // BLOCK)
TILES = BLOCKS * BLOCK_TILES
SLOTS = 4
ROUNDS = BLOCKS // SLOTS
ROUND_TILES = SLOTS * BLOCK_TILES
GATHERED = 16 * BLOCK_TILES
GROUP = 7
GROUPS = WINDOWS // GROUP
HEAD = 6 * GROUP
PAIRS = HEAD // 2
SUB = 16
SUBS = HEAD * P // SUB
JOINT = SUB * WINDOWS
MAIN = 3
EXTRA = 2
COUNT_MAX = 16
GCN_LAYERS = 3
PASSES = GCN_LAYERS + 1
EPS = 1e-5
assert BLOCKS % SLOTS == 0 and WINDOWS % GROUP == 0 and GROUPS % 2 == 0 and HEAD % 2 == 0
def PROJECT(p):
    return 2 * p


def COLLECT(p):
    return 2 * p + 1


POST = 2 * GCN_LAYERS + 1


def gnn_program(nc, x, src, dst, radial, W1, b1, W2, b2, W3, b3, W_pre, b_pre, W_rad, b_rad, W_post, b_post, out):
    ctx = ExitStack()
    with ctx:
        def sbuf(name, shape, dt=F32):
            return ctx.enter_context(nc.sbuf_tensor(name, shape, dt))

        def sem(name):
            return ctx.enter_context(nc.semaphore(name))

        def cut(buffer, at, n):
            return buffer[:, at:at + n]

        table = nc.dram_tensor("table", (PAD_NODES, D), F32, kind="Internal").ap()
        table_pw = table.rearrange("(p w) f -> p w f", w=WINDOWS)
        counts = nc.dram_tensor("counts", (HEAD, P, WINDOWS * P // 4), F32, kind="Internal").ap()

        row_i = sbuf("row_i", [P, TILES], I32)
        dst_rel = sbuf("dst_rel", [P, TILES])
        row_stage = sbuf("row_stage", [P, ROUND_TILES], I32)
        node = sbuf("node", [P, WINDOWS, D])
        joint_flat = node[:, :, :].rearrange("p w f -> p (w f)").bitcast(F16)
        joint_hot = [joint_flat[:, k * JOINT:(k + 1) * JOINT] for k in range(2 * MAIN + EXTRA)]
        sumT = sbuf("sumT", [D, SUMS])

        wide = sbuf("wide", [P, WINDOWS * 3 * D // 2])
        xs = cut(wide, 0, WINDOWS * D).rearrange("p (w f) -> p w f", f=D)
        src_rem = cut(wide, WINDOWS * D, TILES // 2).bitcast(F16)
        joint_of = cut(wide, WINDOWS * D + TILES, TILES)
        parts = wide[:, :].bitcast(BF16).rearrange("p (w n) -> p w n", n=3 * D)

        ring = sbuf("ring", [P, 4 * TILES])
        src_i = cut(ring, 0, TILES).bitcast(I32)
        dst_i = cut(ring, TILES, TILES).bitcast(I32)
        dst_rem = cut(ring, 2 * TILES, TILES // 2).bitcast(BF16)
        dst_win = cut(ring, 3 * TILES, TILES // 2).bitcast(BF16)
        count_bytes = ring[:, :].rearrange("p (h n) -> p h n", h=2)
        count_ring = ring[:, :].bitcast(F8).rearrange("p (h q n) -> p h q n", h=2, n=P)
        radial_sb = ring[0:RADIAL + 1, 0:SLOTS * BLOCK].rearrange("p (j e) -> p j e", j=SLOTS)

        hot = sbuf("hot", [P, 2 * BLOCK_TILES * SPAN])
        onehot = hot[:, :].rearrange("p (a k n) -> p a k n", a=2, n=SPAN)
        rem_hot = cut(hot, 0, BLOCK_TILES * P).bitcast(BF16).rearrange("p (a n k) -> p a n k", a=2, n=P)
        win_hot = cut(hot, BLOCK_TILES * P, BLOCK_TILES * WINDOWS).bitcast(BF16).rearrange(
            "p (a n k) -> p a n k", a=2, n=WINDOWS)
        src_hot = [cut(hot, a * MAIN * P // 2, MAIN * P // 2).bitcast(F16).rearrange("p (n k) -> p n k", n=P)
                   for a in range(3)]
        unused = [cut(hot, 3 * MAIN * P // 2 + a * JOINT // 2, JOINT // 2).bitcast(BF16) for a in range(2)]
        onehot_more = sbuf("onehot_more", [P, BLOCK_TILES, MORE])
        more_flat = onehot_more[:, :, :].rearrange("p k n -> p (k n)")
        iota_block = cut(more_flat, 0, P * BLOCK_TILES // 2).bitcast(BF16).rearrange("p (n k) -> p n k", n=P)
        iota_main = cut(more_flat, P * BLOCK_TILES // 2, P * MAIN // 2).bitcast(F16).rearrange("p (n k) -> p n k", n=P)
        rel_more = sbuf("rel_more", [P, BLOCK_TILES])
        joint_rel = sbuf("joint_rel", [P, 3, MAIN])

        rows_flat = sbuf("rows_flat", [P, SLOTS * BLOCK_TILES * D])
        rows = rows_flat[:, :].rearrange("p (j n) -> p j n", j=SLOTS)
        iota_joint = cut(rows_flat, 0, JOINT // 2).bitcast(F16)
        sub_start = cut(rows_flat, JOINT, SUBS)

        msg_flat = sbuf("msg_flat", [P, 2 * BLOCK_TILES * D])
        msg = msg_flat[:, :].rearrange("p (a n) -> p a n", a=2)
        range_p = cut(msg_flat, 0, 2 * BLOCKS)
        range_p1 = cut(msg_flat, 2 * BLOCKS, 2 * BLOCKS)

        stage_nf = sbuf("stage_nf", [P, GROUP, D])
        stage_fn = sbuf("stage_fn", [D, 2, GROUP * P])
        sub_count = stage_fn[0:1, 0, 0:SUBS]
        sub_end = stage_fn[0:1, 0, SUBS:2 * SUBS]
        sub_tmp = stage_fn[0:1, 1, 0:SUBS]
        sub_i = stage_fn[0:1, 1, SUBS:2 * SUBS].bitcast(I32)
        tmp = sbuf("tmp", [P, GROUP, D])
        iota_i = tmp[:, :, :].rearrange("p w f -> p (w f)").bitcast(I32)
        iota = sbuf("iota", [P, SPAN])
        ident = sbuf("ident", [P, P])
        pick = sbuf("pick", [P, P // SUB])
        start = sbuf("start", [P, WINDOWS])
        zeros16 = sbuf("zeros16", [P, P], F16)
        less_max = sbuf("less_max", [P, 1])
        span_f = sbuf("span_f", [1, BLOCKS])
        block_no = sbuf("block_no", [1, BLOCKS])
        span_i = sbuf("span_i", [1, BLOCKS], I32)
        base = sbuf("base", [1, BLOCKS], I32)
        more = sbuf("more", [1, BLOCKS], I32)
        sub_tile = sbuf("sub_tile", [1, SUBS], I32)
        sub_more = sbuf("sub_more", [1, SUBS], I32)
        found = sbuf("found", [P, SUBS])
        found_ring = sbuf("found_ring", [P, 2, P // SUB])
        excess = sbuf("excess", [P, SUBS])
        check_p = sbuf("check_p", [P, 3])
        check = sbuf("check", [P, 3])
        mode_f = sbuf("mode_f", [1, 4])
        mode = sbuf("mode", [1, 4], I32)
        gate = sbuf("gate", [P, GROUPS])
        deg = sbuf("deg", [P, WINDOWS])
        root = sbuf("root", [P, WINDOWS])
        dinv = sbuf("dinv", [P, WINDOWS])
        mean = sbuf("mean", [P, WINDOWS])
        var = sbuf("var", [P, WINDOWS])
        std = sbuf("std", [P, WINDOWS])
        rstd = sbuf("rstd", [P, WINDOWS])
        dense_sum = sbuf("dense_sum", [P, 2, D])
        w_gcn = [sbuf(f"w_gcn{i}", [D, D]) for i in range(GCN_LAYERS)]
        w_pre = sbuf("w_pre", [D, D])
        w_rad = sbuf("w_rad", [RADIAL + 1, D])
        w_post = sbuf("w_post", [D, D])
        bias = sbuf("bias", [P, 5, D])
        B_PRE, B_POST = 3, 4

        ps = ctx.enter_context(nc.psum_tensor("ps", [P, 8, 512], F32))
        ps_sum = ps[:, 0:2, :]
        ps_filt = ps[:, 2:4, :]
        ps_dense = ps[:, 2:4, 0:3 * D]
        ps_z = ps[:, 4:6, :]
        ps_more = ps[:, 4, 0:MORE]
        ps_t = ps[:, 6:8, :].rearrange("p a n -> p (a n)")
        ps_deg = ps[:, 0, 0:WINDOWS]
        ps_sub = ps[0:1, 4, 0:P // SUB * HEAD]
        ps_count = [ps[:, 4 * a:4 * a + 4, 0:JOINT // 4] for a in range(2)]

        loaded = sem("loaded")
        xs_cleared = sem("xs_cleared")
        xs_loaded = sem("xs_loaded")
        radial_ones = sem("radial_ones")
        radial_loaded = [sem(f"radial_loaded{j}") for j in range(SLOTS)]
        gathered = [sem(f"gathered{j}") for j in range(SLOTS)]
        gather_turn = sem("gather_turn")
        sp_turn = sem("sp_turn")
        pe_turn = sem("pe_turn")
        act_turn = sem("act_turn")
        dve_turn = sem("dve_turn")
        consts_made = sem("consts_made")
        row_ready = sem("row_ready")
        block_range = sem("block_range")
        range_all = sem("range_all")
        step = sem("step")
        deg_hot = sem("deg_hot")
        deg_used = sem("deg_used")
        deg_ready = sem("deg_ready")
        sub_counted = sem("sub_counted")
        sub_ready = sem("sub_ready")
        main_rel = sem("main_rel")
        main_ready = sem("main_ready")
        main_used = sem("main_used")
        extra_rel = sem("extra_rel")
        extra_ready = sem("extra_ready")
        extra_used = sem("extra_used")
        built = sem("built")
        sub_copied = sem("sub_copied")
        found_kept = sem("found_kept")
        window_full = sem("window_full")
        counts_written = [sem(f"counts_written{h}") for h in range(2)]
        check_ready = sem("check_ready")
        check_all = sem("check_all")
        mode_ready = sem("mode_ready")
        rows_staged = sem("rows_staged")
        slot_free = sem("slot_free")
        onehot_ready = sem("onehot_ready")
        summed = sem("summed")
        more_rel = sem("more_rel")
        more_ready = sem("more_ready")
        more_summed = sem("more_summed")
        more_added = sem("more_added")
        counts_loaded = [sem(f"counts_loaded{h}") for h in range(2)]
        parts_ready = sem("parts_ready")
        dense_ready = sem("dense_ready")
        dense_summed = sem("dense_summed")
        dense_taken = sem("dense_taken")
        filter_ready = sem("filter_ready")
        msg_ready = sem("msg_ready")
        root_wanted = sem("root_wanted")
        root_ready = sem("root_ready")
        sums_done = sem("sums_done")
        h_ready = sem("h_ready")
        nf_staged = sem("nf_staged")
        flipped = sem("flipped")
        fn_staged = sem("fn_staged")
        z_ready = sem("z_ready")
        z_used = sem("z_used")
        table_written = sem("table_written")
        y_ready = sem("y_ready")
        exp_ready = sem("exp_ready")
        out_ready = sem("out_ready")
        out_written = sem("out_written")

        N_LOADS = 4 + 5 + 5 + 2
        N_CONSTS = 11

        def groups(g, n=1):
            return bass.ds(g * GROUP, n * GROUP)

        def nodes(g):
            return bass.ds(g * (GROUP * P), GROUP * P)

        def over_features(column):
            return column.unsqueeze(2).to_broadcast((P, column.shape[1], D))

        def over_windows(row, n):
            return row.unsqueeze(1).to_broadcast((P, n, D))

        class Pass:

            def __init__(self, eng, p):
                low = ROUNDS - 2
                if p < GCN_LAYERS:
                    self.first = eng.value_load(mode[0:1, 0:1], min_val=0, max_val=low)
                    self.rounds = eng.value_load(mode[0:1, 1:2], min_val=2, max_val=ROUNDS)
                    self.pairs = eng.value_load(mode[0:1, 2:3], min_val=0, max_val=PAIRS)
                    self.before = eng.snap(self.rounds * p) if p else 0
                else:
                    gcn = eng.value_load(mode[0:1, 1:2], min_val=2, max_val=ROUNDS)
                    self.first, self.rounds, self.pairs = 0, ROUNDS, None
                    self.before = eng.snap(gcn * GCN_LAYERS)

            def round(self, i):
                if self.pairs is None:
                    return i
                return nc.s_assert_within(i + self.first, 0, ROUNDS - 1,
                                          skip_runtime_bounds_check_because="first + rounds is ROUNDS")

            def block(self, i, j):
                return self.round(i) * SLOTS + j

            def turn(self, i, j):
                return (i + self.before) * SLOTS + j

            def gathers(self, i):
                return (i + self.before) * GATHERED + GATHERED

        block = ctx.enter_context(nc.Block())

        @block.sync
        def _(sp):
            def load_x(arrived, cleared):
                sp.dma_start(xs[:, 0:WINDOWS - 1, :],
                             x[0:(WINDOWS - 1) * P, :].rearrange("(w p) f -> p w f", p=P)).then_inc(arrived, 16)
                sp.wait_ge(xs_cleared, cleared)
                sp.dma_start(xs[0:LAST, WINDOWS - 1, :], x[(WINDOWS - 1) * P:NODES, :]).then_inc(arrived, 16)

            sp.dma_start(dst_i, dst).then_inc(loaded, 16)
            sp.dma_start(src_i, src).then_inc(loaded, 16)
            load_x(loaded, 1)
            for w_sb, w in zip(w_gcn + [w_pre, w_post], (W1, W2, W3, W_pre, W_post)):
                sp.dma_start(w_sb[:, :], w).then_inc(loaded, 16)
            for i, b in enumerate((b1, b2, b3, b_pre, b_post)):
                sp.dma_start(bias[:, i, :], b.to_broadcast((P, D))).then_inc(loaded, 16)
            sp.dma_start(w_rad[0:RADIAL, :], W_rad).then_inc(loaded, 16)
            sp.dma_start(w_rad[RADIAL:RADIAL + 1, :], b_rad).then_inc(loaded, 16)

            with sp.Fori(0, PAIRS) as i:
                for h in range(2):
                    sp.wait_ge(window_full, i * 2 + (h + 1))
                    sp.sem_inc(sp_turn, 1)
                    sp.dma_start(counts[bass.ds(i * 2 + h, 1), :, :].rearrange("a p n -> p (a n)"),
                                 count_bytes[:, h, :]).then_inc(counts_written[h], 16)

            def write_table(p):
                with sp.Fori(0, GROUPS) as g:
                    sp.wait_ge(z_used, g + (PROJECT(p) * GROUPS + 3))
                    sp.dma_start(table_pw[:, groups(g), :], node[:, groups(g), :]).then_inc(table_written, 16)

            sp.wait_ge(mode_ready, 1)
            sp.wait_ge(counts_written[0], 16 * (PAIRS + 1))
            sp.wait_ge(counts_written[1], 16 * (PAIRS + 1))
            for p in range(GCN_LAYERS):
                write_table(p)
                pairs = sp.value_load(mode[0:1, 2:3], min_val=0, max_val=PAIRS)
                with sp.If(pairs > 0):
                    with sp.Fori(0, pairs) as i:
                        for h in range(2):
                            sp.wait_ge(dense_taken, i * 2 + (p * HEAD + h + 1))
                            sp.sem_inc(sp_turn, 1)
                            sp.dma_start(count_bytes[:, h, :],
                                         counts[bass.ds(i * 2 + h, 1), :, :].rearrange("a p n -> p (a n)")
                                         ).then_inc(counts_loaded[h], 16)
            sp.wait_ge(sums_done, GCN_LAYERS)
            load_x(xs_loaded, 2)
            sp.wait_ge(radial_ones, 1)
            for j in range(SLOTS):
                sp.dma_start(radial_sb[0:RADIAL, j, :],
                             radial[:, j * BLOCK:(j + 1) * BLOCK]).then_inc(radial_loaded[j], 16)
            write_table(GCN_LAYERS)
            with sp.Fori(1, ROUNDS) as r:
                for j in range(SLOTS):
                    sp.wait_ge(filter_ready, r * SLOTS + (j + 1 - SLOTS))
                    sp.dma_start(radial_sb[0:RADIAL, j, :],
                                 radial[:, bass.ds(r * (SLOTS * BLOCK) + j * BLOCK, BLOCK)]
                                 ).then_inc(radial_loaded[j], 16)

            with sp.Fori(0, GROUPS - 1) as g:
                sp.wait_ge(out_ready, g + 2)
                sp.dma_start(out[nodes(g), :].rearrange("(w p) f -> p w f", p=P),
                             node[:, groups(g), :]).then_inc(out_written, 16)
            sp.wait_ge(out_ready, GROUPS + 1)
            first = (GROUPS - 1) * GROUP
            sp.dma_start(out[first * P:(WINDOWS - 1) * P, :].rearrange("(w p) f -> p w f", p=P),
                         node[:, first:WINDOWS - 1, :]).then_inc(out_written, 16)
            sp.dma_start(out[(WINDOWS - 1) * P:NODES, :], node[0:LAST, WINDOWS - 1, :]).then_inc(out_written, 16)
            sp.wait_ge(out_written, 16 * (GROUPS + 1))

        @block.gpsimd
        def _(pool):
            nc.gpsimd.memset(xs[:, WINDOWS - 1, :], 0.0).then_inc(xs_cleared, 1)
            nc.gpsimd.memset(ident[:, :], 0.0).then_inc(consts_made, 1)
            nc.gpsimd.memset(zeros16[:, :], 0.0).then_inc(consts_made, 1)
            nc.gpsimd.memset(less_max[:, :], -float(COUNT_MAX)).then_inc(consts_made, 1)
            nc.gpsimd.iota(iota_i[:, 0:SPAN], pattern=[[1, SPAN]], base=0, channel_multiplier=0).then_inc(consts_made, 1)
            nc.gpsimd.iota(iota_i[:, SPAN:SPAN + WINDOWS], pattern=[[MORE, WINDOWS]], base=SPAN,
                           channel_multiplier=0).then_inc(consts_made, 1)
            nc.gpsimd.iota(iota_joint, pattern=[[1, JOINT]], base=0, channel_multiplier=0,
                           allow_small_or_imprecise_dtypes=True).then_inc(consts_made, 1)
            nc.gpsimd.iota(iota_block, pattern=[[1, P], [0, BLOCK_TILES]], base=0, channel_multiplier=0,
                           allow_small_or_imprecise_dtypes=True).then_inc(consts_made, 1)
            nc.gpsimd.iota(iota_main, pattern=[[1, P], [0, MAIN]], base=0, channel_multiplier=0,
                           allow_small_or_imprecise_dtypes=True).then_inc(consts_made, 1)
            nc.gpsimd.iota(sub_start, pattern=[[-JOINT, SUBS]], base=0, channel_multiplier=0,
                           allow_small_or_imprecise_dtypes=True).then_inc(consts_made, 1)
            nc.gpsimd.iota(block_no[:, :], pattern=[[1, BLOCKS]], base=0, channel_multiplier=0,
                           allow_small_or_imprecise_dtypes=True).then_inc(consts_made, 1)
            pool.wait_ge(consts_made, N_CONSTS - 1)
            nc.gpsimd.affine_select(out=ident[:, :], in_=ident[:, :], compare_op=ALU.not_equal, fill=1.0,
                                    base=0, pattern=[[-1, P]], channel_multiplier=1).then_inc(consts_made, 1)
            pool.wait_ge(block_range, 2)
            nc.gpsimd.partition_all_reduce(range_p1, range_p, P, REDUCE.max).then_inc(range_all, 1)
            pool.wait_ge(check_ready, 3)
            nc.gpsimd.partition_all_reduce(check[:, :], check_p[:, :], P, REDUCE.add).then_inc(check_all, 1)

            pool.wait_ge(mode_ready, 1)
            for p in range(PASSES):
                at = Pass(pool, p)
                pool.wait_ge(table_written, 16 * GROUPS * (p + 1))
                with pool.Fori(0, at.rounds) as i:
                    for j in range(SLOTS):
                        pool.wait_ge(rows_staged, at.turn(i, j + 1))
                        pool.sem_inc(gather_turn, 1)
                        for k in range(BLOCK_TILES):
                            c = j * BLOCK_TILES + k
                            nc.gpsimd.indirect_dma_start(
                                out=rows[:, j, k * D:(k + 1) * D], out_offset=None, in_=table[:, :],
                                in_offset=bass.IndirectOffsetOnAxis(ap=row_stage[:, c:c + 1], axis=0),
                            ).then_inc(gathered[j], 16)
                if p == GCN_LAYERS - 1:
                    pool.wait_ge(sums_done, GCN_LAYERS)
                    nc.gpsimd.memset(radial_sb[:, :, :], 1.0).then_inc(radial_ones, 1)

        @block.scalar
        def _(act):
            def square_root(n, to, of):
                act.wait_ge(root_wanted, n + 1)
                nc.scalar.activation(to, of, ACT.Sqrt).then_inc(root_ready, 1)

            def project(p):
                with act.Fori(0, GROUPS // 2) as g2:
                    for h in range(2):
                        g = g2 * 2 + h
                        act.wait_ge(h_ready, g2 * 2 + (p * GROUPS + h + 1))
                        nc.scalar.activation(stage_nf[:, :, :], node[:, groups(g), :], ACT.Relu).then_inc(nf_staged, 1)
                        act.wait_ge(flipped, g2 * 2 + (p * GROUPS + h + 1))
                        nc.scalar.copy(stage_fn[:, h, :], ps_t[0:D, 0:GROUP * P]).then_inc(fn_staged, 1)

            def stage_sums(s, g2, h):
                act.wait_ge(z_ready, g2 * 2 + (s * GROUPS + h - 1))
                nc.scalar.copy(stage_fn[:, h, :], sumT[:, nodes(g2 * 2 + h)]).then_inc(fn_staged, 1)

            act.sem_inc(sub_copied, 2)
            for h in range(2):
                act.sem_inc(counts_written[h], 16)
            square_root(0, root[:, :], deg[:, :])
            act.wait_ge(consts_made, N_CONSTS)
            with act.Fori(0, PAIRS) as i:
                for h in range(2):
                    act.wait_ge(counts_written[h], i * 16 + 16)
                    for s in range(P // SUB):
                        sub = i * (2 * P // SUB) + (h * (P // SUB) + s)
                        act.wait_ge(built, i * (2 * P // SUB) + (h * (P // SUB) + s + 1))
                        act.sem_inc(act_turn, 1)
                        of = ps_count[s % 2].rearrange("p a (d q) -> p a d q", q=WINDOWS)
                        to = count_ring[:, h, :, s * SUB:(s + 1) * SUB].rearrange("p q (a d) -> p a d q", a=4)
                        copied = nc.scalar.activation(to, of, ACT.Identity, saturate=True,
                                                      accum_out=found_ring[:, h, s:s + 1])
                        if s == P // SUB - 1:
                            copied.then_inc(window_full, 1)
                        act.wait_ge(sub_copied, i * (2 * P // SUB) + (h * (P // SUB) + s + 1))
                        nc.scalar.activation(unused[s % 2].rearrange("p (a n) -> p a n", a=4), ps_count[s % 2], ACT.Relu,
                                             bias=less_max[:, :],
                                             accum_out=excess[:, bass.ds(sub, 1)]).then_inc(sub_copied, 1)
                    act.wait_ge(window_full, i * 2 + (h + 1))
                    nc.scalar.copy(found[:, bass.ds(i * (2 * P // SUB) + h * (P // SUB), P // SUB)],
                                   found_ring[:, h, :]).then_inc(found_kept, 1)
            square_root(1, std[:, :], var[:, :])

            act.wait_ge(row_ready, 1)
            act.wait_ge(mode_ready, 1)
            for p in range(PASSES):
                project(p)
                at = Pass(act, p)
                with act.Fori(0, at.rounds) as i:
                    for j in range(SLOTS):
                        act.wait_ge(slot_free, at.turn(i, j + 1))
                        nc.scalar.copy(row_stage[:, j * BLOCK_TILES:(j + 1) * BLOCK_TILES],
                                       row_i[:, bass.ds(at.round(i) * ROUND_TILES + j * BLOCK_TILES, BLOCK_TILES)]
                                       ).then_inc(rows_staged, 1)
                act.wait_ge(sums_done, p + 1)
                if p < GCN_LAYERS:
                    with act.Fori(0, GROUPS // 2) as g2:
                        for h in range(2):
                            stage_sums(COLLECT(p), g2, h)
                if p == GCN_LAYERS - 1:
                    square_root(2, std[:, :], var[:, :])
            with act.Fori(0, GROUPS // 2) as g2:
                for h in range(2):
                    stage_sums(POST, g2, h)
                    act.wait_ge(y_ready, g2 * 2 + (h + 1))
                    nc.scalar.activation(tmp[:, :, :], tmp[:, :, :], ACT.Exp, scale=-1.0).then_inc(exp_ready, 1)

        @block.vector
        def _(dve):
            steps = [0]

            def then(ins):
                ins.then_inc(step, 1)
                steps[0] += 1

            def settle():
                dve.wait_ge(step, steps[0])

            def layernorm(n):
                then(nc.vector.tensor_reduce(mean[:, :], xs, AX.X, ALU.add))
                settle()
                then(nc.vector.tensor_scalar(mean[:, :], mean[:, :], 1.0 / D, None, ALU.mult))
                settle()
                then(nc.vector.tensor_tensor(node[:, :, :], xs, over_features(mean[:, :]), ALU.subtract))
                settle()
                at = steps[0]
                with dve.Fori(0, GROUPS) as g:
                    dve.wait_ge(step, g * 2 + at)
                    nc.vector.tensor_tensor(tmp[:, :, :], node[:, groups(g), :], node[:, groups(g), :],
                                            ALU.mult).then_inc(step, 1)
                    dve.wait_ge(step, g * 2 + (at + 1))
                    nc.vector.tensor_reduce(var[:, groups(g)], tmp[:, :, :], AX.X, ALU.add).then_inc(step, 1)
                steps[0] += 2 * GROUPS
                settle()
                nc.vector.tensor_scalar(var[:, :], var[:, :], 1.0 / D, EPS, ALU.mult, ALU.add).then_inc(root_wanted, 1)
                dve.wait_ge(root_ready, n)
                then(nc.vector.reciprocal(rstd[:, :], std[:, :]))
                settle()
                nc.vector.tensor_tensor(node[:, :, :], node[:, :, :], over_features(rstd[:, :]),
                                        ALU.mult).then_inc(h_ready, GROUPS)

            def one_hot(to, columns, tile0, rel):
                for k in range(BLOCK_TILES):
                    one = nc.vector.tensor_scalar(to[:, k, :], columns, rel[:, bass.ds(tile0 + k, 1)], None,
                                                  ALU.is_equal)
                return one

            def tile_hots(to, columns, of):
                return nc.vector.tensor_tensor(to, columns, of.unsqueeze(1).to_broadcast(to.shape), ALU.is_equal)

            def add_sum(at, i, j):
                dve.wait_ge(summed, at.turn(i, j + 3))
                first = dve.value_load(base[0:1, bass.ds(at.block(i, j), 1)], min_val=0, max_val=NODES)
                to = sumT[:, bass.ds(first, SPAN)]
                dve.wait_ge(slot_free, at.turn(i, j + SLOTS))
                nc.vector.tensor_tensor(to, to, ps_sum[0:D, j % 2, 0:SPAN], ALU.add).then_inc(slot_free, 1)

            def add_more(at, i, j):
                n = dve.value_load(more[0:1, bass.ds(at.block(i, j), 1)], min_val=0, max_val=WINDOWS)
                with dve.If(n > 0):
                    first = dve.value_load(base[0:1, bass.ds(at.block(i, j), 1)], min_val=0, max_val=NODES)
                    dve.wait_ge(slot_free, at.turn(i, j + SLOTS))
                    dve.sem_inc(dve_turn, 1)
                    with dve.Fori(0, n) as m:
                        nc.vector.tensor_scalar(rel_more[:, :], dst_rel[:, bass.ds(at.block(i, j) * BLOCK_TILES, BLOCK_TILES)],
                                                start[:, bass.ds(m, 1)], None, ALU.subtract).then_inc(more_rel, 1)
                        dve.wait_ge(more_rel, dve.snap(count))
                        one_hot(onehot_more, iota[:, 0:MORE], 0, rel_more).then_inc(more_ready, 1)
                        dve.wait_ge(more_summed, dve.snap(count))
                        start_at = nc.s_assert_within(
                            first + (m * MORE + SPAN), 0, NODES,
                            skip_runtime_bounds_check_because="it is at most the largest destination")
                        to = sumT[:, bass.ds(start_at, MORE)]
                        nc.vector.tensor_tensor(to, to, ps_more[0:D, :], ALU.add).then_inc(more_added, 1)
                        dve.wait_ge(more_added, dve.snap(count))
                        dve.reg_add(count, count, 1)

            def take_dense(p, i):
                for h in range(2):
                    dve.wait_ge(dense_ready, i * 2 + (p * HEAD + h + 1))
                    nc.vector.tensor_reduce(dense_sum[:, h, :], ps_dense[:, h, :].rearrange("p (c f) -> p f c", c=3),
                                            AX.X, ALU.add).then_inc(dense_summed, 1)
                    dve.wait_ge(dense_summed, i * 2 + (p * HEAD + h + 1))
                    pair = nc.s_assert_within(i, 0, PAIRS - 1, skip_runtime_bounds_check_because="it is under pairs")
                    mine = node[:, bass.ds(pair * 2 + h, 1), :].rearrange("p a f -> p (a f)")
                    nc.vector.tensor_tensor(mine, mine, dense_sum[:, h, :], ALU.add).then_inc(dense_taken, 1)

            def edge_pass(p):
                at = Pass(dve, p)
                with dve.Fori(0, at.rounds) as i:
                    for j in range(SLOTS):
                        dve.wait_ge(summed, at.turn(i, j + 1))
                        one_hot(onehot[:, j % 2, :, :], iota[:, :], at.block(i, j) * BLOCK_TILES,
                                dst_rel).then_inc(onehot_ready, 1)
                        if p == GCN_LAYERS:
                            dve.wait_ge(filter_ready, i * SLOTS + (j + 1))
                            dve.wait_ge(gathered[j], at.gathers(i))
                            nc.vector.tensor_tensor(msg[:, j % 2, :], rows[:, j, :], ps_filt[:, j % 2, :],
                                                    ALU.mult).then_inc(msg_ready, 1)
                        if j:
                            add_sum(at, i, j - 1)
                        add_more(at, i, j)
                        if j == 2 and p < GCN_LAYERS:
                            with dve.If(i * 2 < at.pairs):
                                take_dense(p, i * 2)
                    add_sum(at, i, SLOTS - 1)
                    if p < GCN_LAYERS:
                        with dve.If(i * 2 + 1 < at.pairs):
                            take_dense(p, i * 2 + 1)
                if p < GCN_LAYERS:
                    with dve.If(at.rounds * 2 < at.pairs):
                        with dve.Fori(at.rounds * 2, at.pairs) as i:
                            take_dense(p, i)
                dve.drain().then_inc(sums_done, 1)

            dve.sem_inc(slot_free, SLOTS)
            dve.sem_inc(dense_taken, 2)
            dve.sem_inc(z_used, 2)
            dve.sem_inc(out_ready, 1)
            dve.wait_ge(loaded, 16 * N_LOADS)
            dve.wait_ge(consts_made, N_CONSTS)
            then(nc.vector.tensor_copy(dst_rel[:, :], dst_i))
            then(nc.vector.tensor_copy(iota[:, :], iota_i[:, 0:SPAN]))
            then(nc.vector.tensor_copy(start[:, :], iota_i[:, SPAN:SPAN + WINDOWS]))
            then(nc.vector.tensor_single_scalar(row_i[:, :], dst_i, P - 1, ALU.bitwise_and))
            settle()
            then(nc.vector.tensor_copy(dst_rem, row_i[:, :]))
            then(nc.vector.tensor_single_scalar(dst_i, dst_i, 7, ALU.logical_shift_right))
            settle()
            then(nc.vector.tensor_copy(dst_win, dst_i))
            by_block = dst_rel[:, :].rearrange("p (b k) -> p b k", k=BLOCK_TILES)
            nc.vector.tensor_reduce(range_p[:, 0:BLOCKS], by_block, AX.X, ALU.min, negate=True).then_inc(block_range, 1)
            nc.vector.tensor_reduce(range_p[:, BLOCKS:], by_block, AX.X, ALU.max).then_inc(block_range, 1)
            settle()
            then(nc.vector.tensor_single_scalar(row_i[:, :], src_i, P - 1, ALU.bitwise_and))
            then(nc.vector.tensor_single_scalar(dst_i, src_i, 7, ALU.logical_shift_right))
            settle()
            then(nc.vector.tensor_copy(src_rem, row_i[:, :]))
            then(nc.vector.scalar_tensor_tensor(joint_of, dst_rel[:, :], float(WINDOWS), dst_i, ALU.mult, ALU.add))
            settle()
            nc.vector.scalar_tensor_tensor(row_i[:, :], row_i[:, :], float(WINDOWS), dst_i,
                                           ALU.mult, ALU.add).then_inc(row_ready, 1)
            then(nc.vector.tensor_reduce(pick[:, :], ident[:, :].rearrange("p (s n) -> p s n", n=SUB), AX.X, ALU.add))

            with dve.Fori(0, BLOCKS // 2) as b2:
                for a in range(2):
                    dve.wait_ge(deg_used, b2 * 2 + (a + 1))
                    tiles = bass.ds(b2 * (2 * BLOCK_TILES) + a * BLOCK_TILES, BLOCK_TILES)
                    tile_hots(rem_hot[:, a, :, :], iota_block, dst_rem[:, tiles])
                    tile_hots(win_hot[:, a, :, :], iota_block[:, 0:WINDOWS, :], dst_win[:, tiles]).then_inc(deg_hot, 1)

            dve.wait_ge(range_all, 1)
            then(nc.vector.tensor_scalar(range_p1[:, 0:BLOCKS], range_p1[:, 0:BLOCKS], -1.0, None, ALU.mult))
            settle()
            then(nc.vector.tensor_copy(base[:, :], range_p1[0:1, 0:BLOCKS]))
            then(nc.vector.tensor_tensor(by_block, by_block,
                                         range_p1[:, 0:BLOCKS].unsqueeze(2).to_broadcast((P, BLOCKS, BLOCK_TILES)),
                                         ALU.subtract))
            then(nc.vector.tensor_tensor(span_f[:, :], range_p1[0:1, BLOCKS:], range_p1[0:1, 0:BLOCKS], ALU.subtract))
            settle()
            then(nc.vector.tensor_scalar(span_f[:, :], span_f[:, :], float(MORE - SPAN), 0.0, ALU.add, ALU.max))
            settle()
            then(nc.vector.tensor_copy(span_i[:, :], span_f[:, :]))
            settle()
            then(nc.vector.memset(sumT[:, :], 0.0))
            then(nc.vector.tensor_single_scalar(more[:, :], span_i[:, :], MORE.bit_length() - 1, ALU.logical_shift_right))
            then(nc.vector.tensor_scalar(span_f[:, :], range_p1[0:1, BLOCKS:], float(HEAD * P), float(4 * BLOCKS),
                                         ALU.is_lt, ALU.mult))
            settle()
            then(nc.vector.tensor_tensor(span_f[:, :], span_f[:, :], block_no[:, :], ALU.add))
            settle()
            then(nc.vector.tensor_reduce(mode_f[:, 3:4], span_f[:, :], AX.X, ALU.min))

            dve.wait_ge(deg_used, BLOCKS + 2)
            nc.vector.tensor_copy(deg[:, :], ps_deg).then_inc(deg_ready, 1)
            dve.wait_ge(sub_counted, 1)
            then(nc.vector.tensor_copy(sub_count.rearrange("a (w s) -> a s w", s=P // SUB),
                                       ps_sub.rearrange("a (s w) -> a s w", w=HEAD)))
            settle()
            then(nc.vector.memset(sub_tmp, 0.0))
            settle()
            then(nc.vector.tensor_tensor_scan(sub_end, sub_count, sub_tmp, 0.0, ALU.add, ALU.add))
            settle()

            def shifted(to, of):
                then(nc.vector.tensor_copy(sub_i, of))
                settle()
                then(nc.vector.tensor_single_scalar(to, sub_i, 7, ALU.logical_shift_right))
                settle()

            then(nc.vector.tensor_tensor(sub_tmp, sub_end, sub_count, ALU.subtract))
            settle()
            shifted(sub_tile[:, :], sub_tmp)
            then(nc.vector.tensor_scalar(sub_tmp, sub_end, -1.0, 0.0, ALU.add, ALU.max))
            settle()
            shifted(sub_more[:, :], sub_tmp)
            then(nc.vector.tensor_tensor(sub_tmp, sub_more[:, :], sub_tile[:, :], ALU.subtract))
            settle()
            then(nc.vector.tensor_scalar(sub_tmp, sub_tmp, float(1 - MAIN + EXTRA - 1), 0.0, ALU.add, ALU.max))
            settle()
            then(nc.vector.tensor_copy(sub_i, sub_tmp))
            settle()
            nc.vector.tensor_single_scalar(sub_more[:, :], sub_i, EXTRA.bit_length() - 1,
                                           ALU.logical_shift_right).then_inc(sub_ready, 1)
            nc.vector.tensor_reduce(check_p[:, 2:3], deg[:, 0:HEAD], AX.X, ALU.add).then_inc(check_ready, 1)
            dve.wait_ge(check_ready, 1)
            nc.vector.tensor_scalar(deg[:, :], deg[:, :], 1.0, None, ALU.add).then_inc(root_wanted, 1)
            dve.wait_ge(root_ready, 1)
            then(nc.vector.reciprocal(dinv[:, :], root[:, :]))

            extra_turn = dve.alloc_register("dve_extra")
            dve.reg_mov(extra_turn, 1)
            extra_step = dve.alloc_register("dve_extra_step")
            dve.reg_mov(extra_step, 1)
            dve.wait_ge(sub_ready, 1)
            with dve.Fori(0, SUBS // 2) as s2:
                for a in range(2):
                    sub = s2 * 2 + a
                    t0 = dve.value_load(sub_tile[0:1, bass.ds(sub, 1)], min_val=0, max_val=EDGES // P)
                    n = dve.value_load(sub_more[0:1, bass.ds(sub, 1)], min_val=0, max_val=TILES // EXTRA)
                    dve.wait_ge(main_used, s2 * 2 + (a + 1))
                    nc.vector.tensor_scalar(joint_rel[:, a, :], joint_of[:, bass.ds(t0, MAIN)],
                                            sub_start[:, bass.ds(sub, 1)], None, ALU.add).then_inc(main_rel, 1)
                    tile_hots(src_hot[a], iota_main, src_rem[:, bass.ds(t0, MAIN)])
                    dve.wait_ge(main_rel, s2 * 2 + (a + 1))
                    for k in range(MAIN):
                        made = nc.vector.tensor_scalar(joint_hot[a * MAIN + k], iota_joint, joint_rel[:, a, k:k + 1],
                                                       None, ALU.is_equal)
                    made.then_inc(main_ready, 1)
                    with dve.If(n > 0):
                        with dve.Fori(0, n) as m:
                            t = nc.s_assert_within(
                                t0 + (m * EXTRA + MAIN), 0, TILES - EXTRA,
                                skip_runtime_bounds_check_because="an edge of the head lies in the tile, and "
                                                                  "the last EXTRA tiles hold none")
                            turn = dve.snap(extra_turn, min_val=1, max_val=1 << 16)
                            dve.wait_ge(extra_used, dve.snap(turn + (EXTRA - 1)))
                            nc.vector.tensor_scalar(joint_rel[:, 2, 0:EXTRA], joint_of[:, bass.ds(t, EXTRA)],
                                                    sub_start[:, bass.ds(sub, 1)], None, ALU.add).then_inc(extra_rel, 1)
                            tile_hots(src_hot[2][:, :, 0:EXTRA], iota_main[:, :, 0:EXTRA], src_rem[:, bass.ds(t, EXTRA)])
                            dve.wait_ge(extra_rel, dve.snap(extra_step))
                            for k in range(EXTRA):
                                nc.vector.tensor_scalar(joint_hot[2 * MAIN + k], iota_joint, joint_rel[:, 2, k:k + 1],
                                                        None, ALU.is_equal).then_inc(extra_ready, 1)
                            dve.reg_add(extra_turn, extra_turn, EXTRA)
                            dve.reg_add(extra_step, extra_step, 1)

            dve.wait_ge(sub_copied, SUBS + 2)
            dve.wait_ge(found_kept, HEAD)
            nc.vector.tensor_reduce(check_p[:, 0:1], found[:, :], AX.X, ALU.add).then_inc(check_ready, 1)
            nc.vector.tensor_reduce(check_p[:, 1:2], excess[:, :], AX.X, ALU.add).then_inc(check_ready, 1)
            layernorm(2)
            dve.wait_ge(check_all, 1)
            then(nc.vector.tensor_tensor(mean[:, 0:1], check[:, 0:1], check[:, 2:3], ALU.is_equal))
            then(nc.vector.tensor_scalar(mean[:, 1:2], check[:, 1:2], 0.0, None, ALU.is_equal))
            settle()
            then(nc.vector.tensor_tensor(mean[:, 2:3], mean[:, 0:1], mean[:, 1:2], ALU.mult))
            settle()
            then(nc.vector.memset(gate[:, HEAD // GROUP:], 1.0))
            then(nc.vector.tensor_scalar(gate[:, 0:HEAD // GROUP], mean[:, 2:3].to_broadcast((P, HEAD // GROUP)),
                                         -1.0, 1.0, ALU.mult, ALU.add))
            then(nc.vector.tensor_copy(mode[:, 3:4], mode_f[:, 3:4]))
            settle()
            then(nc.vector.tensor_single_scalar(mode[:, 3:4], mode[:, 3:4], SLOTS.bit_length() - 1,
                                                ALU.logical_shift_right))
            settle()
            then(nc.vector.tensor_scalar(mode_f[:, 0:1], mode[:, 3:4], float(ROUNDS - 2), mean[0:1, 2:3],
                                         ALU.min, ALU.mult))
            then(nc.vector.tensor_scalar(mode_f[:, 2:3], mean[0:1, 2:3], float(PAIRS), None, ALU.mult))
            settle()
            then(nc.vector.tensor_scalar(mode_f[:, 1:2], mode_f[:, 0:1], -1.0, float(ROUNDS), ALU.mult, ALU.add))
            settle()
            nc.vector.tensor_copy(mode[:, 0:3], mode_f[:, 0:3]).then_inc(mode_ready, 1)
            dve.wait_ge(mode_ready, 1)

            count = dve.alloc_register("dve_count")
            dve.reg_mov(count, 1)

            def z_of(s, g2, h):
                dve.wait_ge(z_ready, g2 * 2 + (s * GROUPS + h + 1))
                return ps_z[:, h, 0:GROUP * D].rearrange("p (w f) -> p w f", f=D)

            for p in range(PASSES):
                with dve.Fori(0, GROUPS // 2) as g2:
                    for h in range(2):
                        mine = node[:, groups(g2 * 2 + h), :]
                        z = z_of(PROJECT(p), g2, h)
                        if p < GCN_LAYERS:
                            nc.vector.tensor_tensor(mine, z, over_features(dinv[:, groups(g2 * 2 + h)]),
                                                    ALU.mult).then_inc(z_used, 1)
                        else:
                            nc.vector.tensor_tensor(mine, z, over_windows(bias[:, B_PRE, :], GROUP),
                                                    ALU.add).then_inc(z_used, 1)
                if p:
                    then(nc.vector.memset(sumT[:, :], 0.0))
                if p < GCN_LAYERS:
                    at = steps[0]
                    with dve.Fori(0, GROUPS) as g:
                        mine = node[:, groups(g), :]
                        part = [parts[:, groups(g), c * D:(c + 1) * D] for c in range(3)]
                        dve.wait_ge(z_used, (PROJECT(p) + 1) * GROUPS + 2)
                        dve.wait_ge(step, g * 4 + at)
                        nc.vector.tensor_copy(part[0], mine).then_inc(step, 1)
                        dve.wait_ge(step, g * 4 + (at + 1))
                        nc.vector.tensor_tensor(tmp[:, :, :], mine, part[0], ALU.subtract).then_inc(step, 1)
                        dve.wait_ge(step, g * 4 + (at + 2))
                        nc.vector.tensor_copy(part[1], tmp[:, :, :]).then_inc(step, 1)
                        dve.wait_ge(step, g * 4 + (at + 3))
                        nc.vector.tensor_tensor(part[2], tmp[:, :, :], part[1], ALU.subtract).then_inc(step, 1)
                    steps[0] += 4 * GROUPS
                    settle()
                    dve.drain().then_inc(parts_ready, 1)
                    dve.wait_ge(table_written, 16 * GROUPS * (p + 1))
                else:
                    settle()
                edge_pass(p)
                if p == GCN_LAYERS:
                    break

                if p == GCN_LAYERS - 1:
                    then(nc.vector.memset(xs[:, WINDOWS - 1, :], 0.0))
                    settle()
                    dve.drain().then_inc(xs_cleared, 1)
                    dve.wait_ge(xs_loaded, 32)
                at = steps[0]
                n_steps = 1 if p < GCN_LAYERS - 1 else 3
                with dve.Fori(0, GROUPS // 2) as g2:
                    for h in range(2):
                        g = g2 * 2 + h
                        mine = node[:, groups(g), :]
                        z = z_of(COLLECT(p), g2, h)

                        def after(k):
                            dve.wait_ge(step, g2 * (2 * n_steps) + (at + h * n_steps + k))

                        nc.vector.scalar_tensor_tensor(mine, z, gate[:, bass.ds(g, 1)], mine,
                                                       ALU.mult, ALU.add).then_inc(z_used, 1)
                        dve.wait_ge(z_used, g2 * 2 + (COLLECT(p) * GROUPS + h + 3))
                        nc.vector.tensor_tensor(mine, mine, over_features(dinv[:, groups(g)]), ALU.mult).then_inc(step, 1)
                        after(1)
                        b = over_windows(bias[:, p, :], GROUP)
                        if p < GCN_LAYERS - 1:
                            nc.vector.tensor_tensor(mine, mine, b, ALU.add).then_inc(h_ready, 1)
                        else:
                            nc.vector.tensor_tensor(mine, mine, b, ALU.add).then_inc(step, 1)
                            after(2)
                            nc.vector.tensor_tensor(xs[:, groups(g), :], xs[:, groups(g), :], mine, ALU.add).then_inc(step, 1)
                steps[0] += n_steps * GROUPS
                if p == GCN_LAYERS - 1:
                    settle()
                    layernorm(3)

            at = steps[0]
            with dve.Fori(0, GROUPS // 2) as g2:
                for h in range(2):
                    g = g2 * 2 + h
                    mine = node[:, groups(g), :]
                    z = z_of(POST, g2, h)

                    def after(k):
                        dve.wait_ge(step, g2 * 6 + (at + h * 3 + k))

                    nc.vector.tensor_tensor(mine, z, over_windows(bias[:, B_POST, :], GROUP), ALU.add).then_inc(z_used, 1)
                    dve.wait_ge(z_used, g2 * 2 + (POST * GROUPS + h + 3))
                    dve.wait_ge(out_ready, g2 * 2 + (h + 1))
                    nc.vector.tensor_scalar(tmp[:, :, :], mine, -87.0, None, ALU.max).then_inc(y_ready, 1)
                    dve.wait_ge(exp_ready, g2 * 2 + (h + 1))
                    nc.vector.tensor_scalar(tmp[:, :, :], tmp[:, :, :], 1.0, None, ALU.add).then_inc(step, 1)
                    after(1)
                    nc.vector.reciprocal(tmp[:, :, :], tmp[:, :, :]).then_inc(step, 1)
                    after(2)
                    nc.vector.tensor_tensor(tmp[:, :, :], mine, tmp[:, :, :], ALU.mult).then_inc(step, 1)
                    after(3)
                    nc.vector.tensor_tensor(mine, tmp[:, :, :], xs[:, groups(g), :], ALU.add).then_inc(out_ready, 1)

        @block.tensor
        def _(pe):
            def project(p, w):
                s = PROJECT(p)
                with pe.Fori(0, GROUPS // 2) as g2:
                    for h in range(2):
                        pe.wait_ge(nf_staged, g2 * 2 + (p * GROUPS + h + 1))
                        pe.sem_inc(pe_turn, 1)
                        for i in range(GROUP):
                            t = nc.tensor.transpose(ps_t[0:D, i * P:(i + 1) * P], stage_nf[:, i, :], ident[:, :])
                        t.then_inc(flipped, 1)
                        product_z(s, g2, h, w)

            def product_z(s, g2, h, w):
                pe.wait_ge(fn_staged, g2 * 2 + (s * GROUPS + h + 1))
                pe.wait_ge(z_used, g2 * 2 + (s * GROUPS + h + 1))
                for i in range(GROUP):
                    z = nc.tensor.matmul(ps_z[:, h, i * D:(i + 1) * D], stage_fn[:, h, i * P:(i + 1) * P],
                                         w, start=True, stop=True)
                z.then_inc(z_ready, 1)

            def product(to, j, mats, messages):
                for k in range(BLOCK_TILES):
                    of = msg[:, j % 2, k * D:(k + 1) * D] if messages else rows[:, j, k * D:(k + 1) * D]
                    s = nc.tensor.matmul(to, of, mats[:, k, :], start=(k == 0), stop=(k == BLOCK_TILES - 1))
                return s

            def dense_pair(p, i):
                for h in range(2):
                    pe.wait_ge(counts_loaded[h], i * 16 + (16 * p * PAIRS + 16))
                    pe.wait_ge(dense_taken, i * 2 + (p * HEAD + h + 1))
                    pe.sem_inc(pe_turn, 1)
                    for q in range(WINDOWS):
                        d = nc.tensor.matmul(ps_dense[:, h, :], count_ring[:, h, q, :], parts[:, q, :],
                                             start=(q == 0), stop=(q == WINDOWS - 1))
                    d.then_inc(dense_ready, 1)

            def edge_pass(p):
                messages = p == GCN_LAYERS
                at = Pass(pe, p)
                if not messages:
                    pe.wait_ge(parts_ready, p + 1)
                with pe.Fori(0, at.rounds) as i:
                    for j in range(SLOTS):
                        if messages:
                            pe.wait_ge(radial_loaded[j], i * 16 + 16)
                            for k in range(BLOCK_TILES):
                                f = nc.tensor.matmul(ps_filt[:, j % 2, k * D:(k + 1) * D],
                                                     radial_sb[:, j, k * P:(k + 1) * P], w_rad[:, :],
                                                     start=True, stop=True)
                            f.then_inc(filter_ready, 1)
                            pe.wait_ge(msg_ready, i * SLOTS + (j + 1))
                        else:
                            pe.wait_ge(gathered[j], at.gathers(i))
                        pe.wait_ge(slot_free, at.turn(i, j + SLOTS - 1))
                        pe.wait_ge(onehot_ready, at.turn(i, j + 1))
                        product(ps_sum[0:D, j % 2, 0:SPAN], j, onehot[:, j % 2, :, :], messages).then_inc(summed, 1)
                        n = pe.value_load(more[0:1, bass.ds(at.block(i, j), 1)], min_val=0, max_val=WINDOWS)
                        with pe.If(n > 0):
                            with pe.Fori(0, n):
                                pe.wait_ge(more_ready, pe.snap(count))
                                product(ps_more[0:D, :], j, onehot_more, messages).then_inc(more_summed, 1)
                                pe.reg_add(count, count, 1)
                        if j % 2 and not messages:
                            with pe.If(i * 2 + j // 2 < at.pairs):
                                dense_pair(p, i * 2 + j // 2)
                if not messages:
                    with pe.If(at.rounds * 2 < at.pairs):
                        with pe.Fori(at.rounds * 2, at.pairs) as i:
                            dense_pair(p, i)

            pe.sem_inc(deg_used, 2)
            pe.sem_inc(main_used, 2)
            pe.sem_inc(extra_used, EXTRA)
            pe.sem_inc(summed, 2)
            pe.wait_ge(loaded, 16 * N_LOADS)
            pe.wait_ge(consts_made, N_CONSTS)

            def deg_block(b, a, first, last):
                pe.wait_ge(deg_hot, b + 1)
                for k in range(BLOCK_TILES):
                    d = nc.tensor.matmul(ps_deg, rem_hot[:, a, :, k], win_hot[:, a, :, k],
                                         start=(first and k == 0), stop=(last and k == BLOCK_TILES - 1))
                d.then_inc(deg_used, 1)

            deg_block(0, 0, True, False)
            deg_block(1, 1, False, False)
            with pe.Fori(1, BLOCKS // 2 - 1) as b2:
                for a in range(2):
                    deg_block(b2 * 2 + a, a, False, False)
            deg_block(BLOCKS - 2, 0, False, False)
            deg_block(BLOCKS - 1, 1, False, True)
            pe.wait_ge(deg_ready, 1)
            for s in range(P // SUB):
                n = nc.tensor.matmul(ps_sub[:, s * HEAD:(s + 1) * HEAD], pick[:, s:s + 1], deg[:, 0:HEAD],
                                     start=True, stop=True)
            n.then_inc(sub_counted, 1)

            extra_turn = pe.alloc_register("pe_extra")
            pe.reg_mov(extra_turn, 1)

            def joint_tile(to, a, k, slot, first):
                for c in range(4):
                    m = nc.tensor.matmul(to[:, c, :], src_hot[a][:, :, k],
                                         joint_hot[slot][:, c * (JOINT // 4):(c + 1) * (JOINT // 4)],
                                         start=first, stop=True, skip_group_check=not first)
                return m

            pe.wait_ge(sub_ready, 1)
            with pe.Fori(0, SUBS // 2) as s2:
                for a in range(2):
                    n = pe.value_load(sub_more[0:1, bass.ds(s2 * 2 + a, 1)], min_val=0, max_val=TILES // EXTRA)
                    pe.wait_ge(sub_copied, s2 * 2 + (a + 1))
                    pe.wait_ge(main_ready, s2 * 2 + (a + 1))
                    pe.sem_inc(pe_turn, 1)
                    for k in range(MAIN):
                        m = joint_tile(ps_count[a], a, k, a * MAIN + k, k == 0)
                    m.then_inc(main_used, 1)
                    with pe.If(n > 0):
                        with pe.Fori(0, n):
                            for k in range(EXTRA):
                                pe.wait_ge(extra_ready, pe.snap(extra_turn))
                                joint_tile(ps_count[a], 2, k, 2 * MAIN + k, False).then_inc(extra_used, 1)
                                pe.reg_add(extra_turn, extra_turn, 1)
                    nc.tensor.matmul(ps_count[a][:, 3, 0:1], zeros16[:, :], zeros16[:, 0:1],
                                     start=False, stop=True, skip_group_check=True).then_inc(built, 1)

            pe.wait_ge(mode_ready, 1)
            count = pe.alloc_register("pe_count")
            pe.reg_mov(count, 1)
            for p in range(PASSES):
                project(p, (w_gcn + [w_pre])[p][:, :])
                edge_pass(p)
                if p < GCN_LAYERS:
                    with pe.Fori(0, GROUPS // 2) as g2:
                        for h in range(2):
                            product_z(COLLECT(p), g2, h, ident[0:D, 0:D])
            with pe.Fori(0, GROUPS // 2) as g2:
                for h in range(2):
                    product_z(POST, g2, h, w_post[:, :])


def kernel(x, src, dst, edge_attr_50, L0_gnn_W1, L0_gnn_b1, L0_gnn_W2, L0_gnn_b2, L0_gnn_W3, L0_gnn_b3,
           L1_gnn_W_pre, L1_gnn_b_pre, L1_gnn_W_rad, L1_gnn_b_rad, L1_gnn_W_post, L1_gnn_b_post):
    import concourse.bacc as bacc
    from concourse.bass_utils import run_bass_kernel_spmd

    def by_tile(a, fill):
        a = np.concatenate([np.asarray(a), np.full(BLOCKS * BLOCK - EDGES, fill, np.int32)])
        return np.ascontiguousarray(a.reshape(TILES, P).T)

    def row(b):
        return np.ascontiguousarray(np.asarray(b).reshape(1, -1))

    def turned(w):
        return np.ascontiguousarray(np.asarray(w).T)

    radial = np.zeros((RADIAL, BLOCKS * BLOCK), np.float32)
    radial[:, :EDGES] = np.asarray(edge_attr_50).T
    arrays = {
        "x": np.ascontiguousarray(x),
        "src": by_tile(src, 0),
        "dst": by_tile(dst, NODES),
        "radial": radial,
        "W1": np.ascontiguousarray(L0_gnn_W1), "b1": row(L0_gnn_b1),
        "W2": np.ascontiguousarray(L0_gnn_W2), "b2": row(L0_gnn_b2),
        "W3": np.ascontiguousarray(L0_gnn_W3), "b3": row(L0_gnn_b3),
        "W_pre": turned(L1_gnn_W_pre), "b_pre": row(L1_gnn_b_pre),
        "W_rad": turned(L1_gnn_W_rad), "b_rad": row(L1_gnn_b_rad),
        "W_post": turned(L1_gnn_W_post), "b_post": row(L1_gnn_b_post),
    }
    nc = bacc.Bacc("TRN2", target_bir_lowering=False, num_devices=1)
    args = {name: nc.dram_tensor(f"in_{name}", a.shape, mybir.dt.from_np(a.dtype), kind="ExternalInput").ap()
            for name, a in arrays.items()}
    out = nc.dram_tensor("out", (NODES, D), F32, kind="ExternalOutput").ap()
    gnn_program(nc, out=out, **args)
    result = run_bass_kernel_spmd(nc, [{f"in_{name}": a for name, a in arrays.items()}], core_ids=[0])
    return result.results[0]["out"]
```

```python
from contextlib import ExitStack

import concourse.bass as bass
import numpy as np
from concourse import mybir

F32 = mybir.dt.float32
BF16 = mybir.dt.bfloat16
F16 = mybir.dt.float16
F8 = mybir.dt.float8e4
I32 = mybir.dt.int32
ALU = mybir.AluOpType
ACT = mybir.ActivationFunctionType
AX = mybir.AxisListType
REDUCE = bass.bass_isa.ReduceOp

P = 128
NODES, EDGES, D, RADIAL = 12500, 200000, 64, 50
WINDOWS = -(-NODES // P)
LAST = NODES - (WINDOWS - 1) * P
PAD_NODES = WINDOWS * P
SPAN = 160
MORE = 128
SUMS = PAD_NODES + SPAN
BLOCK_TILES = 8
BLOCK = BLOCK_TILES * P
BLOCKS = -(-EDGES // BLOCK)
TILES = BLOCKS * BLOCK_TILES
SLOTS = 4
ROUNDS = BLOCKS // SLOTS
ROUND_TILES = SLOTS * BLOCK_TILES
GATHERED = 16 * BLOCK_TILES
GROUP = 7
GROUPS = WINDOWS // GROUP
HEAD = 38
PAIRS = HEAD // 2
SUB = 16
SUBS = HEAD * P // SUB
JOINT = SUB * WINDOWS
MAIN = 3
EXTRA = 2
COUNT_MAX = 16
GCN_LAYERS = 3
PASSES = GCN_LAYERS + 1
EPS = 1e-5
assert BLOCKS % SLOTS == 0 and WINDOWS % GROUP == 0 and GROUPS % 2 == 0 and HEAD % 2 == 0
def PROJECT(p):
    return 2 * p


def COLLECT(p):
    return 2 * p + 1


POST = 2 * GCN_LAYERS + 1


def gnn_program(nc, x, src, dst, radial, W1, b1, W2, b2, W3, b3, W_pre, b_pre, W_rad, b_rad, W_post, b_post, out):
    ctx = ExitStack()
    with ctx:
        def sbuf(name, shape, dt=F32):
            return ctx.enter_context(nc.sbuf_tensor(name, shape, dt))

        def sem(name):
            return ctx.enter_context(nc.semaphore(name))

        def cut(buffer, at, n):
            return buffer[:, at:at + n]

        table = nc.dram_tensor("table", (PAD_NODES, D), F32, kind="Internal").ap()
        table_pw = table.rearrange("(p w) f -> p w f", w=WINDOWS)
        counts = nc.dram_tensor("counts", (HEAD, P, WINDOWS * P // 4), F32, kind="Internal").ap()

        row_i = sbuf("row_i", [P, TILES], I32)
        dst_rel = sbuf("dst_rel", [P, TILES])
        row_stage = sbuf("row_stage", [P, ROUND_TILES], I32)
        node = sbuf("node", [P, WINDOWS, D])
        joint_flat = node[:, :, :].rearrange("p w f -> p (w f)").bitcast(F16)
        joint_main = [[joint_flat[:, k * JOINT:(k + 1) * JOINT] for k in range(a * MAIN, (a + 1) * MAIN)]
                      for a in range(2)]
        sumT = sbuf("sumT", [P, SUMS])

        wide = sbuf("wide", [P, WINDOWS * 3 * D // 2])
        xs = cut(wide, 0, WINDOWS * D).rearrange("p (w f) -> p w f", f=D)
        src_rem = cut(wide, WINDOWS * D, TILES // 2).bitcast(F16)
        joint_of = cut(wide, WINDOWS * D + TILES, TILES)
        parts = wide[:, :].bitcast(BF16).rearrange("p (w n) -> p w n", n=3 * D)

        ring = sbuf("ring", [P, 4 * TILES])
        src_i = cut(ring, 0, TILES).bitcast(I32)
        dst_i = cut(ring, TILES, TILES).bitcast(I32)
        dst_rem = cut(ring, 2 * TILES, TILES // 2).bitcast(BF16)
        dst_win = cut(ring, 3 * TILES, TILES // 2).bitcast(BF16)
        count_bytes = ring[:, :].rearrange("p (h n) -> p h n", h=2)
        count_ring = ring[:, :].bitcast(F8).rearrange("p (h q n) -> p h q n", h=2, n=P)
        radial_sb = ring[0:RADIAL + 1, 0:SLOTS * BLOCK].rearrange("p (j e) -> p j e", j=SLOTS)

        hot = sbuf("hot", [P, 2 * BLOCK_TILES * SPAN])
        onehot = hot[:, :].rearrange("p (a k n) -> p a k n", a=2, n=SPAN)
        onehot16 = cut(hot, 0, BLOCK_TILES * SPAN).bitcast(BF16).rearrange("p (a k n) -> p a k n", a=2, n=SPAN)
        rest = cut(hot, BLOCK_TILES * SPAN, BLOCK_TILES * D).rearrange("p (k f) -> p k f", f=D)
        rem_hot = cut(hot, 0, BLOCK_TILES * P).bitcast(BF16).rearrange("p (a n k) -> p a n k", a=2, n=P)
        win_hot = cut(hot, BLOCK_TILES * P, BLOCK_TILES * WINDOWS).bitcast(BF16).rearrange(
            "p (a n k) -> p a n k", a=2, n=WINDOWS)
        src_main = [cut(hot, a * MAIN * P // 2, MAIN * P // 2).bitcast(F16).rearrange("p (n k) -> p n k", n=P)
                    for a in range(2)]
        src_extra = [cut(hot, MAIN * P + a * EXTRA * P // 2, EXTRA * P // 2).bitcast(F16).rearrange("p (n k) -> p n k", n=P)
                     for a in range(2)]
        unused = [cut(hot, (MAIN + EXTRA) * P + a * JOINT // 2, JOINT // 2).bitcast(BF16) for a in range(2)]
        stage_nf = cut(hot, 0, 2 * GROUP * D).rearrange("p (h w f) -> p h w f", h=2, f=D)
        gated = stage_nf
        onehot_more = sbuf("onehot_more", [P, BLOCK_TILES, MORE])
        more_flat = onehot_more[:, :, :].rearrange("p k n -> p (k n)")
        iota_block = cut(more_flat, 0, P * BLOCK_TILES // 2).bitcast(BF16).rearrange("p (n k) -> p n k", n=P)
        iota_main = cut(more_flat, P * BLOCK_TILES // 2, P * MAIN // 2).bitcast(F16).rearrange("p (n k) -> p n k", n=P)
        rel_more = sbuf("rel_more", [P, BLOCK_TILES])
        joint_rel = sbuf("joint_rel", [P, 4, MAIN])

        rows_flat = sbuf("rows_flat", [P, SLOTS * BLOCK_TILES * D])
        rows = rows_flat[:, :].rearrange("p (j n) -> p j n", j=SLOTS)
        iota_joint = cut(rows_flat, 0, JOINT // 2).bitcast(F16)
        sub_start = cut(rows_flat, JOINT // 2, SUBS)

        msg_flat = sbuf("msg_flat", [P, 2 * BLOCK_TILES * D])
        msg = msg_flat[:, :].rearrange("p (a n) -> p a n", a=2)
        split = [words.bitcast(BF16) for words in (cut(hot, BLOCK_TILES * (SPAN + D), BLOCK_TILES * 3 * D // 2),
                                                   cut(msg_flat, 0, BLOCK_TILES * 3 * D // 2))]
        split_upper = [s[:, 0:BLOCK_TILES * 2 * D].rearrange("p (k n) -> p k n", n=2 * D) for s in split]
        split_low = [s[:, BLOCK_TILES * 2 * D:].rearrange("p (k n) -> p k n", n=D) for s in split]
        range_p = cut(msg_flat, 0, 2 * BLOCKS)
        range_p1 = cut(msg_flat, 2 * BLOCKS, 2 * BLOCKS)
        joint_extra = [[joint_flat[:, k * JOINT:(k + 1) * JOINT] for k in range(2 * MAIN, 2 * MAIN + EXTRA)],
                       [cut(msg_flat, 0, JOINT // 2).bitcast(F16),
                        cut(rows_flat, JOINT // 2 + SUBS, JOINT // 2).bitcast(F16)]]

        stage_fn = sbuf("stage_fn", [P, 2, GROUP * P])
        sub_count = stage_fn[0:1, 0, 0:SUBS]
        sub_end = stage_fn[0:1, 0, SUBS:2 * SUBS]
        sub_tmp = stage_fn[0:1, 1, 0:SUBS]
        sub_i = stage_fn[0:1, 1, SUBS:2 * SUBS].bitcast(I32)
        tmp = sbuf("tmp", [P, GROUP, D])
        iota_i = tmp[:, :, :].rearrange("p w f -> p (w f)").bitcast(I32)
        iota = sbuf("iota", [P, SPAN])
        iota16 = sbuf("iota16", [P, SPAN], BF16)
        ident = sbuf("ident", [P, P])
        both_halves = sbuf("both_halves", [P, D])
        pick = sbuf("pick", [P, P // SUB])
        start = sbuf("start", [P, WINDOWS])
        zeros16 = sbuf("zeros16", [P, P], F16)
        less_max = sbuf("less_max", [P, 1])
        one = sbuf("one", [P, 1])
        span_f = sbuf("span_f", [1, BLOCKS])
        block_no = sbuf("block_no", [1, BLOCKS])
        span_i = sbuf("span_i", [1, BLOCKS], I32)
        base = sbuf("base", [1, BLOCKS], I32)
        more = sbuf("more", [1, BLOCKS], I32)
        sub_tile = sbuf("sub_tile", [1, SUBS], I32)
        sub_more = sbuf("sub_more", [1, SUBS], I32)
        found = sbuf("found", [P, SUBS])
        found_ring = sbuf("found_ring", [P, 2, P // SUB])
        excess = sbuf("excess", [P, SUBS])
        check_p = sbuf("check_p", [P, 3])
        check = sbuf("check", [P, 3])
        mode_f = sbuf("mode_f", [1, 4])
        mode = sbuf("mode", [1, 4], I32)
        gate = sbuf("gate", [P, 1])
        deg = sbuf("deg", [P, WINDOWS])
        root = sbuf("root", [P, WINDOWS])
        dinv = sbuf("dinv", [P, WINDOWS])
        mean = sbuf("mean", [P, WINDOWS])
        var = sbuf("var", [P, WINDOWS])
        std = sbuf("std", [P, WINDOWS])
        rstd = sbuf("rstd", [P, WINDOWS])
        dense_sum = sbuf("dense_sum", [P, 2, D])
        w_gcn = [sbuf(f"w_gcn{i}", [D, D]) for i in range(GCN_LAYERS)]
        w_pre = sbuf("w_pre", [D, D])
        w_rad = sbuf("w_rad", [RADIAL + 1, D])
        w_post = sbuf("w_post", [D, D])
        bias = sbuf("bias", [P, 5, D])
        B_PRE, B_POST = 3, 4

        ps = ctx.enter_context(nc.psum_tensor("ps", [P, 8, 512], F32))
        ps_sum = ps[:, 0:2, :]
        ps_filt = ps[:, 2:4, :]
        ps_dense = ps[:, 2:4, 0:3 * D]
        ps_z = ps[:, 4:6, :]
        ps_more = ps[:, 4, 0:MORE]
        ps_t = [ps[:, a:a + 2, :].rearrange("p a n -> p (a n)") for a in (6, 2)]
        ps_deg = ps[:, 0, 0:WINDOWS]
        ps_sub = ps[0:1, 4, 0:P // SUB * HEAD]
        ps_count = [ps[:, 4 * a:4 * a + 4, 0:JOINT // 4] for a in range(2)]

        loaded = sem("loaded")
        xs_cleared = sem("xs_cleared")
        xs_loaded = sem("xs_loaded")
        radial_ones = sem("radial_ones")
        radial_loaded = [sem(f"radial_loaded{j}") for j in range(SLOTS)]
        gathered = [sem(f"gathered{j}") for j in range(SLOTS)]
        gather_turn = sem("gather_turn")
        sp_turn = sem("sp_turn")
        pe_turn = sem("pe_turn")
        act_turn = sem("act_turn")
        dve_turn = sem("dve_turn")
        consts_made = sem("consts_made")
        row_ready = sem("row_ready")
        block_range = sem("block_range")
        range_all = sem("range_all")
        step = sem("step")
        deg_hot = sem("deg_hot")
        deg_used = sem("deg_used")
        deg_ready = sem("deg_ready")
        sub_counted = sem("sub_counted")
        sub_ready = sem("sub_ready")
        main_rel = sem("main_rel")
        main_ready = sem("main_ready")
        main_used = sem("main_used")
        extra_rel = [sem(f"extra_rel{a}") for a in range(2)]
        extra_ready = [sem(f"extra_ready{a}") for a in range(2)]
        extra_used = [sem(f"extra_used{a}") for a in range(2)]
        built = sem("built")
        sub_copied = sem("sub_copied")
        found_kept = sem("found_kept")
        window_full = sem("window_full")
        counts_written = [sem(f"counts_written{h}") for h in range(2)]
        check_ready = sem("check_ready")
        check_all = sem("check_all")
        mode_ready = sem("mode_ready")
        rows_staged = sem("rows_staged")
        slot_free = sem("slot_free")
        onehot_ready = sem("onehot_ready")
        split_step = sem("split_step")
        split_ready = sem("split_ready")
        summed = sem("summed")
        more_rel = sem("more_rel")
        more_ready = sem("more_ready")
        more_summed = sem("more_summed")
        more_added = sem("more_added")
        counts_loaded = [sem(f"counts_loaded{h}") for h in range(2)]
        parts_ready = sem("parts_ready")
        dense_ready = sem("dense_ready")
        dense_summed = sem("dense_summed")
        dense_taken = sem("dense_taken")
        filter_ready = sem("filter_ready")
        msg_ready = sem("msg_ready")
        root_wanted = sem("root_wanted")
        root_ready = sem("root_ready")
        sums_done = sem("sums_done")
        h_ready = sem("h_ready")
        nf_staged = sem("nf_staged")
        flipped = sem("flipped")
        fn_staged = sem("fn_staged")
        z_ready = sem("z_ready")
        z_used = sem("z_used")
        table_written = sem("table_written")
        y_ready = sem("y_ready")
        exp_made = sem("exp_made")
        exp_ready = sem("exp_ready")
        out_ready = sem("out_ready")
        out_written = sem("out_written")

        N_LOADS = 4 + 5 + 5 + 2
        N_CONSTS = 12

        def groups(g, n=1):
            return bass.ds(g * GROUP, n * GROUP)

        def nodes(g):
            return bass.ds(g * (GROUP * P), GROUP * P)

        def over_features(column):
            return column.unsqueeze(2).to_broadcast((P, column.shape[1], D))

        def over_windows(row, n):
            return row.unsqueeze(1).to_broadcast((P, n, D))

        class Pass:

            def __init__(self, eng, p):
                low = ROUNDS - 2
                if p < GCN_LAYERS:
                    self.first = eng.value_load(mode[0:1, 0:1], min_val=0, max_val=low)
                    self.rounds = eng.value_load(mode[0:1, 1:2], min_val=2, max_val=ROUNDS)
                    self.pairs = eng.value_load(mode[0:1, 2:3], min_val=0, max_val=PAIRS)
                    self.before = eng.snap(self.rounds * p) if p else 0
                else:
                    gcn = eng.value_load(mode[0:1, 1:2], min_val=2, max_val=ROUNDS)
                    self.first, self.rounds, self.pairs = 0, ROUNDS, None
                    self.before = eng.snap(gcn * GCN_LAYERS)

            def round(self, i):
                if self.pairs is None:
                    return i
                return nc.s_assert_within(i + self.first, 0, ROUNDS - 1,
                                          skip_runtime_bounds_check_because="first + rounds is ROUNDS")

            def block(self, i, j):
                return self.round(i) * SLOTS + j

            def turn(self, i, j):
                return (i + self.before) * SLOTS + j

            def gathers(self, i):
                return (i + self.before) * GATHERED + GATHERED

        def below(pair):
            return nc.s_assert_within(pair, 0, PAIRS - 1, skip_runtime_bounds_check_because="it is under pairs")

        def dense_turn(eng, pair_next, end, work, h, last):
            pair = eng.snap(pair_next, min_val=0, max_val=PAIRS)
            with eng.If(pair < end):
                work(below(pair), h)
                if last:
                    eng.reg_add(pair_next, pair_next, 1)

        def dense_rest(eng, pairs, pair_next, work):
            first = eng.snap(pair_next, min_val=0, max_val=PAIRS)
            with eng.If(first < pairs):
                with eng.Fori(first, pairs) as pair:
                    for h in range(2):
                        work(below(pair), h)

        def by_turns(eng, ahead, behind):
            ahead(0, 0)
            with eng.Fori(0, GROUPS // 2 - 1) as g2:
                for h in range(2):
                    ahead(g2 + h, 1 - h)
                    behind(g2, h)
            ahead(GROUPS // 2 - 1, 1)
            behind(GROUPS // 2 - 1, 0)
            behind(GROUPS // 2 - 1, 1)

        block = ctx.enter_context(nc.Block())

        @block.sync
        def _(sp):
            def load_x(arrived, cleared):
                sp.dma_start(xs[:, 0:WINDOWS - 1, :],
                             x[0:(WINDOWS - 1) * P, :].rearrange("(w p) f -> p w f", p=P)).then_inc(arrived, 16)
                sp.wait_ge(xs_cleared, cleared)
                sp.dma_start(xs[0:LAST, WINDOWS - 1, :], x[(WINDOWS - 1) * P:NODES, :]).then_inc(arrived, 16)

            sp.dma_start(dst_i, dst).then_inc(loaded, 16)
            sp.dma_start(src_i, src).then_inc(loaded, 16)
            load_x(loaded, 1)
            for w_sb, w in zip(w_gcn + [w_pre, w_post], (W1, W2, W3, W_pre, W_post)):
                sp.dma_start(w_sb[:, :], w).then_inc(loaded, 16)
            for i, b in enumerate((b1, b2, b3, b_pre, b_post)):
                sp.dma_start(bias[:, i, :], b.to_broadcast((P, D))).then_inc(loaded, 16)
            sp.dma_start(w_rad[0:RADIAL, :], W_rad).then_inc(loaded, 16)
            sp.dma_start(w_rad[RADIAL:RADIAL + 1, :], b_rad).then_inc(loaded, 16)

            with sp.Fori(0, PAIRS) as i:
                for h in range(2):
                    sp.wait_ge(window_full, i * 2 + (h + 1))
                    sp.sem_inc(sp_turn, 1)
                    sp.dma_start(counts[bass.ds(i * 2 + h, 1), :, :].rearrange("a p n -> p (a n)"),
                                 count_bytes[:, h, :]).then_inc(counts_written[h], 16)

            def write_table(p):
                with sp.Fori(0, GROUPS) as g:
                    sp.wait_ge(z_used, g + (PROJECT(p) * GROUPS + 3))
                    sp.dma_start(table_pw[:, groups(g), :], node[:, groups(g), :]).then_inc(table_written, 16)

            sp.wait_ge(mode_ready, 1)
            sp.wait_ge(counts_written[0], 16 * (PAIRS + 1))
            sp.wait_ge(counts_written[1], 16 * (PAIRS + 1))
            for p in range(GCN_LAYERS):
                write_table(p)
                pairs = sp.value_load(mode[0:1, 2:3], min_val=0, max_val=PAIRS)
                with sp.If(pairs > 0):
                    with sp.Fori(0, pairs) as i:
                        for h in range(2):
                            sp.wait_ge(dense_ready, i * 2 + (p * HEAD + h + 1))
                            sp.sem_inc(sp_turn, 1)
                            sp.dma_start(count_bytes[:, h, :],
                                         counts[bass.ds(i * 2 + h, 1), :, :].rearrange("a p n -> p (a n)")
                                         ).then_inc(counts_loaded[h], 16)
            sp.wait_ge(sums_done, GCN_LAYERS)
            load_x(xs_loaded, 2)
            sp.wait_ge(radial_ones, 1)
            for j in range(SLOTS):
                sp.dma_start(radial_sb[0:RADIAL, j, :],
                             radial[:, j * BLOCK:(j + 1) * BLOCK]).then_inc(radial_loaded[j], 16)
            write_table(GCN_LAYERS)
            with sp.Fori(1, ROUNDS) as r:
                for j in range(SLOTS):
                    sp.wait_ge(filter_ready, r * SLOTS + (j + 1 - SLOTS))
                    sp.dma_start(radial_sb[0:RADIAL, j, :],
                                 radial[:, bass.ds(r * (SLOTS * BLOCK) + j * BLOCK, BLOCK)]
                                 ).then_inc(radial_loaded[j], 16)

            with sp.Fori(0, GROUPS - 1) as g:
                sp.wait_ge(out_ready, g + 2)
                sp.dma_start(out[nodes(g), :].rearrange("(w p) f -> p w f", p=P),
                             node[:, groups(g), :]).then_inc(out_written, 16)
            sp.wait_ge(out_ready, GROUPS + 1)
            first = (GROUPS - 1) * GROUP
            sp.dma_start(out[first * P:(WINDOWS - 1) * P, :].rearrange("(w p) f -> p w f", p=P),
                         node[:, first:WINDOWS - 1, :]).then_inc(out_written, 16)
            sp.dma_start(out[(WINDOWS - 1) * P:NODES, :], node[0:LAST, WINDOWS - 1, :]).then_inc(out_written, 16)
            sp.wait_ge(out_written, 16 * (GROUPS + 1))

        @block.gpsimd
        def _(pool):
            nc.gpsimd.memset(xs[:, WINDOWS - 1, :], 0.0).then_inc(xs_cleared, 1)
            nc.gpsimd.memset(ident[:, :], 0.0).then_inc(consts_made, 1)
            nc.gpsimd.memset(zeros16[:, :], 0.0).then_inc(consts_made, 1)
            nc.gpsimd.memset(less_max[:, :], -float(COUNT_MAX)).then_inc(consts_made, 1)
            nc.gpsimd.memset(one[:, :], 1.0).then_inc(consts_made, 1)
            nc.gpsimd.iota(iota_i[:, 0:SPAN], pattern=[[1, SPAN]], base=0, channel_multiplier=0).then_inc(consts_made, 1)
            nc.gpsimd.iota(iota_i[:, SPAN:SPAN + WINDOWS], pattern=[[MORE, WINDOWS]], base=SPAN,
                           channel_multiplier=0).then_inc(consts_made, 1)
            nc.gpsimd.iota(iota_joint, pattern=[[1, JOINT]], base=0, channel_multiplier=0,
                           allow_small_or_imprecise_dtypes=True).then_inc(consts_made, 1)
            nc.gpsimd.iota(iota_block, pattern=[[1, P], [0, BLOCK_TILES]], base=0, channel_multiplier=0,
                           allow_small_or_imprecise_dtypes=True).then_inc(consts_made, 1)
            nc.gpsimd.iota(iota_main, pattern=[[1, P], [0, MAIN]], base=0, channel_multiplier=0,
                           allow_small_or_imprecise_dtypes=True).then_inc(consts_made, 1)
            nc.gpsimd.iota(sub_start, pattern=[[-JOINT, SUBS]], base=0, channel_multiplier=0,
                           allow_small_or_imprecise_dtypes=True).then_inc(consts_made, 1)
            nc.gpsimd.iota(block_no[:, :], pattern=[[1, BLOCKS]], base=0, channel_multiplier=0,
                           allow_small_or_imprecise_dtypes=True).then_inc(consts_made, 1)
            pool.wait_ge(consts_made, N_CONSTS - 1)
            nc.gpsimd.affine_select(out=ident[:, :], in_=ident[:, :], compare_op=ALU.not_equal, fill=1.0,
                                    base=0, pattern=[[-1, P]], channel_multiplier=1).then_inc(consts_made, 1)
            pool.wait_ge(block_range, 2)
            nc.gpsimd.partition_all_reduce(range_p1, range_p, P, REDUCE.max).then_inc(range_all, 1)
            pool.wait_ge(check_ready, 3)
            nc.gpsimd.partition_all_reduce(check[:, :], check_p[:, :], P, REDUCE.add).then_inc(check_all, 1)

            pool.wait_ge(mode_ready, 1)
            for p in range(PASSES):
                at = Pass(pool, p)
                pool.wait_ge(table_written, 16 * GROUPS * (p + 1))
                with pool.Fori(0, at.rounds) as i:
                    for j in range(SLOTS):
                        pool.wait_ge(rows_staged, at.turn(i, j + 1))
                        pool.sem_inc(gather_turn, 1)
                        for k in range(BLOCK_TILES):
                            c = j * BLOCK_TILES + k
                            nc.gpsimd.indirect_dma_start(
                                out=rows[:, j, k * D:(k + 1) * D], out_offset=None, in_=table[:, :],
                                in_offset=bass.IndirectOffsetOnAxis(ap=row_stage[:, c:c + 1], axis=0),
                            ).then_inc(gathered[j], 16)
                if p == GCN_LAYERS - 1:
                    pool.wait_ge(sums_done, GCN_LAYERS)
                    nc.gpsimd.memset(radial_sb[:, :, :], 1.0).then_inc(radial_ones, 1)

        @block.scalar
        def _(act):
            def square_root(n, to, of):
                act.wait_ge(root_wanted, n + 1)
                nc.scalar.activation(to, of, ACT.Sqrt).then_inc(root_ready, 1)

            def project(p):
                def features(g2, h):
                    act.wait_ge(h_ready, g2 * 2 + (p * GROUPS + h + 1))
                    nc.scalar.activation(stage_nf[:, h, :, :], node[:, groups(g2 * 2 + h), :], ACT.Relu).then_inc(nf_staged, 1)

                def transposed(g2, h):
                    act.wait_ge(flipped, g2 * 2 + (p * GROUPS + h + 1))
                    nc.scalar.copy(stage_fn[0:D, h, :], ps_t[h][0:D, 0:GROUP * P]).then_inc(fn_staged, 1)

                by_turns(act, features, transposed)

            def stage_sums(s, g2, h, rows):
                act.wait_ge(z_ready, g2 * 2 + (s * GROUPS + h - 1))
                nc.scalar.copy(stage_fn[0:rows, h, :], sumT[0:rows, nodes(g2 * 2 + h)]).then_inc(fn_staged, 1)

            act.sem_inc(sub_copied, 2)
            for h in range(2):
                act.sem_inc(counts_written[h], 16)
            square_root(0, root[:, :], deg[:, :])
            act.wait_ge(consts_made, N_CONSTS)
            with act.Fori(0, PAIRS) as i:
                for h in range(2):
                    act.wait_ge(counts_written[h], i * 16 + 16)
                    for s in range(P // SUB):
                        sub = i * (2 * P // SUB) + (h * (P // SUB) + s)
                        act.wait_ge(built, i * (2 * P // SUB) + (h * (P // SUB) + s + 1))
                        act.sem_inc(act_turn, 1)
                        of = ps_count[s % 2].rearrange("p a (d q) -> p a d q", q=WINDOWS)
                        to = count_ring[:, h, :, s * SUB:(s + 1) * SUB].rearrange("p q (a d) -> p a d q", a=4)
                        copied = nc.scalar.activation(to, of, ACT.Identity, saturate=True,
                                                      accum_out=found_ring[:, h, s:s + 1])
                        if s == P // SUB - 1:
                            copied.then_inc(window_full, 1)
                        act.wait_ge(sub_copied, i * (2 * P // SUB) + (h * (P // SUB) + s + 1))
                        nc.scalar.activation(unused[s % 2].rearrange("p (a n) -> p a n", a=4), ps_count[s % 2], ACT.Relu,
                                             bias=less_max[:, :],
                                             accum_out=excess[:, bass.ds(sub, 1)]).then_inc(sub_copied, 1)
                    act.wait_ge(window_full, i * 2 + (h + 1))
                    nc.scalar.copy(found[:, bass.ds(i * (2 * P // SUB) + h * (P // SUB), P // SUB)],
                                   found_ring[:, h, :]).then_inc(found_kept, 1)
            square_root(1, std[:, :], var[:, :])

            act.wait_ge(row_ready, 1)
            act.wait_ge(mode_ready, 1)
            for p in range(PASSES):
                project(p)
                at = Pass(act, p)
                with act.Fori(0, at.rounds) as i:
                    for j in range(SLOTS):
                        act.wait_ge(slot_free, at.turn(i, j + 1))
                        nc.scalar.copy(row_stage[:, j * BLOCK_TILES:(j + 1) * BLOCK_TILES],
                                       row_i[:, bass.ds(at.round(i) * ROUND_TILES + j * BLOCK_TILES, BLOCK_TILES)]
                                       ).then_inc(rows_staged, 1)
                act.wait_ge(sums_done, p + 1)
                if p < GCN_LAYERS:
                    with act.Fori(0, GROUPS // 2) as g2:
                        for h in range(2):
                            stage_sums(COLLECT(p), g2, h, P)
                if p == GCN_LAYERS - 1:
                    square_root(2, std[:, :], var[:, :])
            def closing_sums(g2, h):
                stage_sums(POST, g2, h, D)

            def closing_exp(g2, h):
                act.wait_ge(y_ready, g2 * 2 + (h + 1))
                nc.scalar.activation(gated[:, h, :, :], gated[:, h, :, :], ACT.Exp, scale=-1.0).then_inc(exp_made, 1)
                act.wait_ge(exp_made, g2 * 2 + (h + 1))
                nc.scalar.activation(gated[:, h, :, :], gated[:, h, :, :], ACT.Identity,
                                     bias=one[:, :]).then_inc(exp_ready, 1)

            by_turns(act, closing_sums, closing_exp)

        @block.vector
        def _(dve):
            steps = [0]

            def then(ins):
                ins.then_inc(step, 1)
                steps[0] += 1

            def settle():
                dve.wait_ge(step, steps[0])

            def layernorm(n):
                then(nc.vector.tensor_reduce(mean[:, :], xs, AX.X, ALU.add))
                settle()
                then(nc.vector.tensor_scalar(mean[:, :], mean[:, :], 1.0 / D, None, ALU.mult))
                settle()
                then(nc.vector.tensor_tensor(node[:, :, :], xs, over_features(mean[:, :]), ALU.subtract))
                settle()
                at = steps[0]
                with dve.Fori(0, GROUPS) as g:
                    dve.wait_ge(step, g * 2 + at)
                    nc.vector.tensor_tensor(tmp[:, :, :], node[:, groups(g), :], node[:, groups(g), :],
                                            ALU.mult).then_inc(step, 1)
                    dve.wait_ge(step, g * 2 + (at + 1))
                    nc.vector.tensor_reduce(var[:, groups(g)], tmp[:, :, :], AX.X, ALU.add).then_inc(step, 1)
                steps[0] += 2 * GROUPS
                settle()
                nc.vector.tensor_scalar(var[:, :], var[:, :], 1.0 / D, EPS, ALU.mult, ALU.add).then_inc(root_wanted, 1)
                dve.wait_ge(root_ready, n)
                then(nc.vector.reciprocal(rstd[:, :], std[:, :]))
                settle()
                nc.vector.tensor_tensor(node[:, :, :], node[:, :, :], over_features(rstd[:, :]),
                                        ALU.mult).then_inc(h_ready, GROUPS)

            def one_hot(to, columns, tile0, rel):
                for k in range(BLOCK_TILES):
                    one = nc.vector.tensor_scalar(to[:, k, :], columns, rel[:, bass.ds(tile0 + k, 1)], None,
                                                  ALU.is_equal)
                return one

            def tile_hots(to, columns, of):
                return nc.vector.tensor_tensor(to, columns, of.unsqueeze(1).to_broadcast(to.shape), ALU.is_equal)

            def split_rows(at, i, j):
                whole = rows[:, j, :].rearrange("p (k f) -> p k f", f=D)
                high, middle = split_upper[j % 2][:, :, 0:D], split_upper[j % 2][:, :, D:]

                def after(k):
                    dve.wait_ge(split_step, at.turn(i, j) * 3 + k)

                dve.wait_ge(gathered[j], at.gathers(i))
                nc.vector.tensor_copy(high, whole).then_inc(split_step, 1)
                dve.wait_ge(split_ready, at.turn(i, j + 1))
                after(1)
                nc.vector.tensor_tensor(rest, whole, high, ALU.subtract).then_inc(split_step, 1)
                after(2)
                nc.vector.tensor_copy(middle, rest).then_inc(split_step, 1)
                after(3)
                nc.vector.tensor_tensor(split_low[j % 2], rest, middle, ALU.subtract).then_inc(split_ready, 1)

            def add_sum(at, i, j, n):
                dve.wait_ge(summed, at.turn(i, j + 3))
                first = dve.value_load(base[0:1, bass.ds(at.block(i, j), 1)], min_val=0, max_val=NODES)
                to = sumT[0:n, bass.ds(first, SPAN)]
                dve.wait_ge(slot_free, at.turn(i, j + SLOTS))
                nc.vector.tensor_tensor(to, to, ps_sum[0:n, j % 2, 0:SPAN], ALU.add).then_inc(slot_free, 1)

            def add_more(at, i, j):
                n = dve.value_load(more[0:1, bass.ds(at.block(i, j), 1)], min_val=0, max_val=WINDOWS)
                with dve.If(n > 0):
                    first = dve.value_load(base[0:1, bass.ds(at.block(i, j), 1)], min_val=0, max_val=NODES)
                    dve.wait_ge(slot_free, at.turn(i, j + SLOTS))
                    dve.sem_inc(dve_turn, 1)
                    with dve.Fori(0, n) as m:
                        nc.vector.tensor_scalar(rel_more[:, :], dst_rel[:, bass.ds(at.block(i, j) * BLOCK_TILES, BLOCK_TILES)],
                                                start[:, bass.ds(m, 1)], None, ALU.subtract).then_inc(more_rel, 1)
                        dve.wait_ge(more_rel, dve.snap(count))
                        one_hot(onehot_more, iota[:, 0:MORE], 0, rel_more).then_inc(more_ready, 1)
                        dve.wait_ge(more_summed, dve.snap(count))
                        start_at = nc.s_assert_within(
                            first + (m * MORE + SPAN), 0, NODES,
                            skip_runtime_bounds_check_because="it is at most the largest destination")
                        to = sumT[0:D, bass.ds(start_at, MORE)]
                        nc.vector.tensor_tensor(to, to, ps_more[0:D, :], ALU.add).then_inc(more_added, 1)
                        dve.wait_ge(more_added, dve.snap(count))
                        dve.reg_add(count, count, 1)

            def take_dense(p, i, h):
                dve.wait_ge(dense_ready, i * 2 + (p * HEAD + h + 3))
                nc.vector.tensor_reduce(dense_sum[:, h, :], ps_dense[:, h, :].rearrange("p (c f) -> p f c", c=3),
                                        AX.X, ALU.add).then_inc(dense_summed, 1)
                dve.wait_ge(dense_summed, i * 2 + (p * HEAD + h + 1))
                mine = node[:, bass.ds(i * 2 + h, 1), :].rearrange("p a f -> p (a f)")
                nc.vector.tensor_tensor(mine, mine, dense_sum[:, h, :], ALU.add).then_inc(dense_taken, 1)

            def edge_pass(p):
                def take(pair, h):
                    take_dense(p, pair, h)

                at = Pass(dve, p)
                if p < GCN_LAYERS:
                    for taken in pair_taken:
                        dve.reg_mov(taken, 0)
                with dve.Fori(0, at.rounds) as i:
                    for j in range(SLOTS):
                        dve.wait_ge(summed, at.turn(i, j + 1))
                        if p < GCN_LAYERS:
                            one_hot(onehot16[:, j % 2, :, :], iota16[:, :], at.block(i, j) * BLOCK_TILES,
                                    dst_rel).then_inc(onehot_ready, 1)
                            split_rows(at, i, j)
                            if j == 3:
                                dense_turn(dve, pair_taken[0], at.pairs, take, 0, True)
                            if j == 1:
                                dense_turn(dve, pair_taken[1], dve.snap(pair_taken[0]), take, 1, True)
                        else:
                            one_hot(onehot[:, j % 2, :, :], iota[:, :], at.block(i, j) * BLOCK_TILES,
                                    dst_rel).then_inc(onehot_ready, 1)
                            dve.wait_ge(filter_ready, i * SLOTS + (j + 1))
                            dve.wait_ge(gathered[j], at.gathers(i))
                            nc.vector.tensor_tensor(msg[:, j % 2, :], rows[:, j, :], ps_filt[:, j % 2, :],
                                                    ALU.mult).then_inc(msg_ready, 1)
                        if j:
                            add_sum(at, i, j - 1, P if p < GCN_LAYERS else D)
                        add_more(at, i, j)
                    add_sum(at, i, SLOTS - 1, P if p < GCN_LAYERS else D)
                if p < GCN_LAYERS:
                    dense_turn(dve, pair_taken[1], dve.snap(pair_taken[0]), take, 1, True)
                    dense_rest(dve, at.pairs, pair_taken[0], take)
                    dve.wait_ge(slot_free, at.turn(at.rounds, SLOTS))
                    nc.vector.tensor_scalar(sumT[:, 0:HEAD * P], sumT[:, 0:HEAD * P], gate[:, 0:1], None,
                                            ALU.mult)
                dve.drain().then_inc(sums_done, 1)

            dve.sem_inc(slot_free, SLOTS)
            dve.sem_inc(dense_taken, 2)
            dve.sem_inc(z_used, 2)
            dve.sem_inc(out_ready, 1)
            dve.wait_ge(loaded, 16 * N_LOADS)
            dve.wait_ge(consts_made, N_CONSTS)
            then(nc.vector.tensor_copy(dst_rel[:, :], dst_i))
            then(nc.vector.tensor_copy(iota[:, :], iota_i[:, 0:SPAN]))
            then(nc.vector.tensor_copy(iota16[:, :], iota_i[:, 0:SPAN]))
            then(nc.vector.tensor_tensor(both_halves[:, :], ident[:, 0:D], ident[:, D:], ALU.add))
            then(nc.vector.tensor_copy(start[:, :], iota_i[:, SPAN:SPAN + WINDOWS]))
            then(nc.vector.tensor_single_scalar(row_i[:, :], dst_i, P - 1, ALU.bitwise_and))
            settle()
            then(nc.vector.tensor_copy(dst_rem, row_i[:, :]))
            then(nc.vector.tensor_single_scalar(dst_i, dst_i, 7, ALU.logical_shift_right))
            settle()
            then(nc.vector.tensor_copy(dst_win, dst_i))
            by_block = dst_rel[:, :].rearrange("p (b k) -> p b k", k=BLOCK_TILES)
            nc.vector.tensor_reduce(range_p[:, 0:BLOCKS], by_block, AX.X, ALU.min, negate=True).then_inc(block_range, 1)
            nc.vector.tensor_reduce(range_p[:, BLOCKS:], by_block, AX.X, ALU.max).then_inc(block_range, 1)
            settle()
            then(nc.vector.tensor_single_scalar(row_i[:, :], src_i, P - 1, ALU.bitwise_and))
            then(nc.vector.tensor_single_scalar(dst_i, src_i, 7, ALU.logical_shift_right))
            settle()
            then(nc.vector.tensor_copy(src_rem, row_i[:, :]))
            then(nc.vector.scalar_tensor_tensor(joint_of, dst_rel[:, :], float(WINDOWS), dst_i, ALU.mult, ALU.add))
            settle()
            nc.vector.scalar_tensor_tensor(row_i[:, :], row_i[:, :], float(WINDOWS), dst_i,
                                           ALU.mult, ALU.add).then_inc(row_ready, 1)
            then(nc.vector.tensor_reduce(pick[:, :], ident[:, :].rearrange("p (s n) -> p s n", n=SUB), AX.X, ALU.add))

            with dve.Fori(0, BLOCKS // 2) as b2:
                for a in range(2):
                    dve.wait_ge(deg_used, b2 * 2 + (a + 1))
                    tiles = bass.ds(b2 * (2 * BLOCK_TILES) + a * BLOCK_TILES, BLOCK_TILES)
                    tile_hots(rem_hot[:, a, :, :], iota_block, dst_rem[:, tiles])
                    tile_hots(win_hot[:, a, :, :], iota_block[:, 0:WINDOWS, :], dst_win[:, tiles]).then_inc(deg_hot, 1)

            dve.wait_ge(range_all, 1)
            then(nc.vector.tensor_scalar(range_p1[:, 0:BLOCKS], range_p1[:, 0:BLOCKS], -1.0, None, ALU.mult))
            settle()
            then(nc.vector.tensor_copy(base[:, :], range_p1[0:1, 0:BLOCKS]))
            then(nc.vector.tensor_tensor(by_block, by_block,
                                         range_p1[:, 0:BLOCKS].unsqueeze(2).to_broadcast((P, BLOCKS, BLOCK_TILES)),
                                         ALU.subtract))
            then(nc.vector.tensor_tensor(span_f[:, :], range_p1[0:1, BLOCKS:], range_p1[0:1, 0:BLOCKS], ALU.subtract))
            settle()
            then(nc.vector.tensor_scalar(span_f[:, :], span_f[:, :], float(MORE - SPAN), 0.0, ALU.add, ALU.max))
            settle()
            then(nc.vector.tensor_copy(span_i[:, :], span_f[:, :]))
            settle()
            then(nc.vector.memset(sumT[:, :], 0.0))
            then(nc.vector.tensor_single_scalar(more[:, :], span_i[:, :], MORE.bit_length() - 1, ALU.logical_shift_right))
            then(nc.vector.tensor_scalar(span_f[:, :], range_p1[0:1, BLOCKS:], float(HEAD * P), float(4 * BLOCKS),
                                         ALU.is_lt, ALU.mult))
            settle()
            then(nc.vector.tensor_tensor(span_f[:, :], span_f[:, :], block_no[:, :], ALU.add))
            settle()
            then(nc.vector.tensor_reduce(mode_f[:, 3:4], span_f[:, :], AX.X, ALU.min))

            dve.wait_ge(deg_used, BLOCKS + 2)
            nc.vector.tensor_copy(deg[:, :], ps_deg).then_inc(deg_ready, 1)
            dve.wait_ge(sub_counted, 1)
            then(nc.vector.tensor_copy(sub_count.rearrange("a (w s) -> a s w", s=P // SUB),
                                       ps_sub.rearrange("a (s w) -> a s w", w=HEAD)))
            settle()
            then(nc.vector.memset(sub_tmp, 0.0))
            settle()
            then(nc.vector.tensor_tensor_scan(sub_end, sub_count, sub_tmp, 0.0, ALU.add, ALU.add))
            settle()

            def shifted(to, of):
                then(nc.vector.tensor_copy(sub_i, of))
                settle()
                then(nc.vector.tensor_single_scalar(to, sub_i, 7, ALU.logical_shift_right))
                settle()

            then(nc.vector.tensor_tensor(sub_tmp, sub_end, sub_count, ALU.subtract))
            settle()
            shifted(sub_tile[:, :], sub_tmp)
            then(nc.vector.tensor_scalar(sub_tmp, sub_end, -1.0, 0.0, ALU.add, ALU.max))
            settle()
            shifted(sub_more[:, :], sub_tmp)
            then(nc.vector.tensor_tensor(sub_tmp, sub_more[:, :], sub_tile[:, :], ALU.subtract))
            settle()
            then(nc.vector.tensor_scalar(sub_tmp, sub_tmp, float(1 - MAIN + EXTRA - 1), 0.0, ALU.add, ALU.max))
            settle()
            then(nc.vector.tensor_copy(sub_i, sub_tmp))
            settle()
            nc.vector.tensor_single_scalar(sub_more[:, :], sub_i, EXTRA.bit_length() - 1,
                                           ALU.logical_shift_right).then_inc(sub_ready, 1)
            nc.vector.tensor_reduce(check_p[:, 2:3], deg[:, 0:HEAD], AX.X, ALU.add).then_inc(check_ready, 1)
            dve.wait_ge(check_ready, 1)
            nc.vector.tensor_scalar(deg[:, :], deg[:, :], 1.0, None, ALU.add).then_inc(root_wanted, 1)
            dve.wait_ge(root_ready, 1)
            then(nc.vector.reciprocal(dinv[:, :], root[:, :]))

            extra_turn = [dve.alloc_register(f"dve_extra{a}") for a in range(2)]
            for turn in extra_turn:
                dve.reg_mov(turn, 1)

            def extra_hots(a, sub, t):
                turn = dve.snap(extra_turn[a], min_val=1, max_val=1 << 16)
                dve.wait_ge(extra_used[a], turn)
                nc.vector.tensor_scalar(joint_rel[:, 2 + a, 0:EXTRA], joint_of[:, bass.ds(t, EXTRA)],
                                        sub_start[:, bass.ds(sub, 1)], None, ALU.add).then_inc(extra_rel[a], 1)
                tile_hots(src_extra[a], iota_main[:, :, 0:EXTRA], src_rem[:, bass.ds(t, EXTRA)])
                dve.wait_ge(extra_rel[a], turn)
                for k in range(EXTRA):
                    made = nc.vector.tensor_scalar(joint_extra[a][k], iota_joint, joint_rel[:, 2 + a, k:k + 1],
                                                   None, ALU.is_equal)
                made.then_inc(extra_ready[a], 1)
                dve.reg_add(extra_turn[a], extra_turn[a], 1)

            def extra_tile(t0, step):
                return nc.s_assert_within(
                    t0 + step * EXTRA + MAIN, 0, TILES - EXTRA,
                    skip_runtime_bounds_check_because="an edge of the head lies in the tile, and the last "
                                                      "EXTRA tiles hold none")

            dve.wait_ge(sub_ready, 1)
            with dve.Fori(0, SUBS // 2) as s2:
                for a in range(2):
                    sub = s2 * 2 + a
                    t0 = dve.value_load(sub_tile[0:1, bass.ds(sub, 1)], min_val=0, max_val=EDGES // P)
                    n = dve.value_load(sub_more[0:1, bass.ds(sub, 1)], min_val=0, max_val=TILES // EXTRA)
                    dve.wait_ge(main_used, s2 * 2 + (a + 1))
                    nc.vector.tensor_scalar(joint_rel[:, a, :], joint_of[:, bass.ds(t0, MAIN)],
                                            sub_start[:, bass.ds(sub, 1)], None, ALU.add).then_inc(main_rel, 1)
                    tile_hots(src_main[a], iota_main, src_rem[:, bass.ds(t0, MAIN)])
                    dve.wait_ge(main_rel, s2 * 2 + (a + 1))
                    for k in range(MAIN):
                        made = nc.vector.tensor_scalar(joint_main[a][k], iota_joint, joint_rel[:, a, k:k + 1],
                                                       None, ALU.is_equal)
                    made.then_inc(main_ready, 1)
                    with dve.If(n > 1):
                        with dve.Fori(0, n >> 1) as m2:
                            for b in range(2):
                                extra_hots(b, sub, extra_tile(t0, m2 * 2 + b))
                    with dve.If((n & 1) > 0):
                        extra_hots(0, sub, extra_tile(t0, n - 1))

            dve.wait_ge(sub_copied, SUBS + 2)
            dve.wait_ge(found_kept, HEAD)
            nc.vector.tensor_reduce(check_p[:, 0:1], found[:, :], AX.X, ALU.add).then_inc(check_ready, 1)
            nc.vector.tensor_reduce(check_p[:, 1:2], excess[:, :], AX.X, ALU.add).then_inc(check_ready, 1)
            layernorm(2)
            dve.wait_ge(check_all, 1)
            then(nc.vector.tensor_tensor(mean[:, 0:1], check[:, 0:1], check[:, 2:3], ALU.is_equal))
            then(nc.vector.tensor_scalar(mean[:, 1:2], check[:, 1:2], 0.0, None, ALU.is_equal))
            settle()
            then(nc.vector.tensor_tensor(mean[:, 2:3], mean[:, 0:1], mean[:, 1:2], ALU.mult))
            settle()
            then(nc.vector.tensor_scalar(gate[:, :], mean[:, 2:3], -1.0, 1.0, ALU.mult, ALU.add))
            then(nc.vector.tensor_copy(mode[:, 3:4], mode_f[:, 3:4]))
            settle()
            then(nc.vector.tensor_single_scalar(mode[:, 3:4], mode[:, 3:4], SLOTS.bit_length() - 1,
                                                ALU.logical_shift_right))
            settle()
            then(nc.vector.tensor_scalar(mode_f[:, 0:1], mode[:, 3:4], float(ROUNDS - 2), mean[0:1, 2:3],
                                         ALU.min, ALU.mult))
            then(nc.vector.tensor_scalar(mode_f[:, 2:3], mean[0:1, 2:3], float(PAIRS), None, ALU.mult))
            settle()
            then(nc.vector.tensor_scalar(mode_f[:, 1:2], mode_f[:, 0:1], -1.0, float(ROUNDS), ALU.mult, ALU.add))
            settle()
            nc.vector.tensor_copy(mode[:, 0:3], mode_f[:, 0:3]).then_inc(mode_ready, 1)
            dve.wait_ge(mode_ready, 1)

            count = dve.alloc_register("dve_count")
            dve.reg_mov(count, 1)
            pair_taken = [dve.alloc_register(f"dve_pair{h}") for h in range(2)]
            dve.sem_inc(split_ready, 1)

            def z_of(s, g2, h):
                dve.wait_ge(z_ready, g2 * 2 + (s * GROUPS + h + 1))
                return ps_z[:, h, 0:GROUP * D].rearrange("p (w f) -> p w f", f=D)

            for p in range(PASSES):
                at = steps[0]
                with dve.Fori(0, GROUPS // 2) as g2:
                    for h in range(2):
                        mine = node[:, groups(g2 * 2 + h), :]
                        z = z_of(PROJECT(p), g2, h)
                        if p < GCN_LAYERS:
                            nc.vector.tensor_tensor(mine, z, over_features(dinv[:, groups(g2 * 2 + h)]),
                                                    ALU.mult).then_inc(z_used, 1)
                            part = [parts[:, groups(g2 * 2 + h), c * D:(c + 1) * D] for c in range(3)]

                            def after(k):
                                dve.wait_ge(step, g2 * 8 + (at + h * 4 + k))

                            dve.wait_ge(z_used, g2 * 2 + (PROJECT(p) * GROUPS + h + 3))
                            after(0)
                            nc.vector.tensor_copy(part[0], mine).then_inc(step, 1)
                            after(1)
                            nc.vector.tensor_tensor(tmp[:, :, :], mine, part[0], ALU.subtract).then_inc(step, 1)
                            after(2)
                            nc.vector.tensor_copy(part[1], tmp[:, :, :]).then_inc(step, 1)
                            after(3)
                            nc.vector.tensor_tensor(part[2], tmp[:, :, :], part[1], ALU.subtract).then_inc(step, 1)
                        else:
                            nc.vector.tensor_tensor(mine, z, over_windows(bias[:, B_PRE, :], GROUP),
                                                    ALU.add).then_inc(z_used, 1)
                if p:
                    then(nc.vector.memset(sumT[:, :], 0.0))
                if p < GCN_LAYERS:
                    steps[0] += 4 * GROUPS
                    settle()
                    dve.drain().then_inc(parts_ready, 1)
                    dve.wait_ge(table_written, 16 * GROUPS * (p + 1))
                else:
                    settle()
                edge_pass(p)
                if p == GCN_LAYERS:
                    break

                if p == GCN_LAYERS - 1:
                    then(nc.vector.memset(xs[:, WINDOWS - 1, :], 0.0))
                    settle()
                    dve.drain().then_inc(xs_cleared, 1)
                    dve.wait_ge(xs_loaded, 32)
                at = steps[0]
                n_steps = 1 if p < GCN_LAYERS - 1 else 3
                with dve.Fori(0, GROUPS // 2) as g2:
                    for h in range(2):
                        g = g2 * 2 + h
                        mine = node[:, groups(g), :]
                        z = z_of(COLLECT(p), g2, h)

                        def after(k):
                            dve.wait_ge(step, g2 * (2 * n_steps) + (at + h * n_steps + k))

                        nc.vector.tensor_tensor(mine, mine, z, ALU.add).then_inc(z_used, 1)
                        dve.wait_ge(z_used, g2 * 2 + (COLLECT(p) * GROUPS + h + 3))
                        nc.vector.tensor_tensor(mine, mine, over_features(dinv[:, groups(g)]), ALU.mult).then_inc(step, 1)
                        after(1)
                        b = over_windows(bias[:, p, :], GROUP)
                        if p < GCN_LAYERS - 1:
                            nc.vector.tensor_tensor(mine, mine, b, ALU.add).then_inc(h_ready, 1)
                        else:
                            nc.vector.tensor_tensor(mine, mine, b, ALU.add).then_inc(step, 1)
                            after(2)
                            nc.vector.tensor_tensor(xs[:, groups(g), :], xs[:, groups(g), :], mine, ALU.add).then_inc(step, 1)
                steps[0] += n_steps * GROUPS
                if p == GCN_LAYERS - 1:
                    settle()
                    layernorm(3)

            at = steps[0]

            def closing_y(g2, h):
                mine = node[:, groups(g2 * 2 + h), :]
                z = z_of(POST, g2, h)
                nc.vector.tensor_tensor(mine, z, over_windows(bias[:, B_POST, :], GROUP), ALU.add).then_inc(z_used, 1)
                dve.wait_ge(z_used, g2 * 2 + (POST * GROUPS + h + 3))
                nc.vector.tensor_scalar(gated[:, h, :, :], mine, -87.0, None, ALU.max).then_inc(y_ready, 1)

            def closing_result(g2, h):
                mine = node[:, groups(g2 * 2 + h), :]
                it = gated[:, h, :, :]

                def after(k):
                    dve.wait_ge(step, g2 * 4 + (at + h * 2 + k))

                dve.wait_ge(exp_ready, g2 * 2 + (h + 1))
                nc.vector.reciprocal(it, it).then_inc(step, 1)
                after(1)
                nc.vector.tensor_tensor(it, mine, it, ALU.mult).then_inc(step, 1)
                after(2)
                nc.vector.tensor_tensor(mine, it, xs[:, groups(g2 * 2 + h), :], ALU.add).then_inc(out_ready, 1)
                dve.wait_ge(out_ready, g2 * 2 + (h + 2))

            by_turns(dve, closing_y, closing_result)

        @block.tensor
        def _(pe):
            def project(p, w):
                s = PROJECT(p)

                def flip(g2, h):
                    pe.wait_ge(nf_staged, g2 * 2 + (p * GROUPS + h + 1))
                    pe.sem_inc(pe_turn, 1)
                    for i in range(GROUP):
                        t = nc.tensor.transpose(ps_t[h][0:D, i * P:(i + 1) * P], stage_nf[:, h, i, :], ident[:, :])
                    t.then_inc(flipped, 1)

                def multiply(g2, h):
                    product_z(s, g2, h, w)

                by_turns(pe, flip, multiply)

            def product_z(s, g2, h, w):
                n = w.shape[0]
                pe.wait_ge(fn_staged, g2 * 2 + (s * GROUPS + h + 1))
                pe.wait_ge(z_used, g2 * 2 + (s * GROUPS + h + 1))
                for i in range(GROUP):
                    z = nc.tensor.matmul(ps_z[:, h, i * D:(i + 1) * D], stage_fn[0:n, h, i * P:(i + 1) * P],
                                         w, start=True, stop=True)
                z.then_inc(z_ready, 1)

            def product(to, j, mats, messages):
                for k in range(BLOCK_TILES):
                    of = msg[:, j % 2, k * D:(k + 1) * D] if messages else rows[:, j, k * D:(k + 1) * D]
                    s = nc.tensor.matmul(to, of, mats[:, k, :], start=(k == 0), stop=(k == BLOCK_TILES - 1))
                return s

            def product_split(to, j):
                for k in range(BLOCK_TILES):
                    mat = onehot16[:, j % 2, k, :]
                    nc.tensor.matmul(to, split_upper[j % 2][:, k, :], mat, start=(k == 0), stop=False,
                                     skip_group_check=True)
                    s = nc.tensor.matmul(to[0:D, :], split_low[j % 2][:, k, :], mat, start=False,
                                         stop=(k == BLOCK_TILES - 1), skip_group_check=True)
                return s

            def dense_window(p, i, h):
                pe.wait_ge(counts_loaded[h], i * 16 + (16 * p * PAIRS + 16))
                pe.wait_ge(dense_taken, i * 2 + (p * HEAD + h + 1))
                pe.sem_inc(pe_turn, 1)
                for q in range(WINDOWS):
                    d = nc.tensor.matmul(ps_dense[:, h, :], count_ring[:, h, q, :], parts[:, q, :],
                                         start=(q == 0), stop=(q == WINDOWS - 1))
                d.then_inc(dense_ready, 1)

            def edge_pass(p):
                def dense(pair, h):
                    dense_window(p, pair, h)

                messages = p == GCN_LAYERS
                at = Pass(pe, p)
                if not messages:
                    pe.wait_ge(parts_ready, p + 1)
                    pe.reg_mov(pair_next, 0)
                with pe.Fori(0, at.rounds) as i:
                    for j in range(SLOTS):
                        if messages:
                            pe.wait_ge(radial_loaded[j], i * 16 + 16)
                            for k in range(BLOCK_TILES):
                                f = nc.tensor.matmul(ps_filt[:, j % 2, k * D:(k + 1) * D],
                                                     radial_sb[:, j, k * P:(k + 1) * P], w_rad[:, :],
                                                     start=True, stop=True)
                            f.then_inc(filter_ready, 1)
                            pe.wait_ge(msg_ready, i * SLOTS + (j + 1))
                        pe.wait_ge(slot_free, at.turn(i, j + SLOTS - 1))
                        pe.wait_ge(onehot_ready, at.turn(i, j + 1))
                        if messages:
                            product(ps_sum[0:D, j % 2, 0:SPAN], j, onehot[:, j % 2, :, :], True).then_inc(summed, 1)
                        else:
                            pe.wait_ge(split_ready, at.turn(i, j + 2))
                            product_split(ps_sum[:, j % 2, 0:SPAN], j).then_inc(summed, 1)
                        n = pe.value_load(more[0:1, bass.ds(at.block(i, j), 1)], min_val=0, max_val=WINDOWS)
                        with pe.If(n > 0):
                            with pe.Fori(0, n):
                                pe.wait_ge(more_ready, pe.snap(count))
                                product(ps_more[0:D, :], j, onehot_more, messages).then_inc(more_summed, 1)
                                pe.reg_add(count, count, 1)
                        if j % 2 and not messages:
                            dense_turn(pe, pair_next, at.pairs, dense, j // 2, j == 3)
                if not messages:
                    dense_rest(pe, at.pairs, pair_next, dense)

            pe.sem_inc(deg_used, 2)
            pe.sem_inc(dense_ready, 2)
            pe.sem_inc(main_used, 2)
            for a in range(2):
                pe.sem_inc(extra_used[a], 1)
            pe.sem_inc(summed, 2)
            pe.wait_ge(loaded, 16 * N_LOADS)
            pe.wait_ge(consts_made, N_CONSTS)

            def deg_block(b, a, first, last):
                pe.wait_ge(deg_hot, b + 1)
                for k in range(BLOCK_TILES):
                    d = nc.tensor.matmul(ps_deg, rem_hot[:, a, :, k], win_hot[:, a, :, k],
                                         start=(first and k == 0), stop=(last and k == BLOCK_TILES - 1))
                d.then_inc(deg_used, 1)

            deg_block(0, 0, True, False)
            deg_block(1, 1, False, False)
            with pe.Fori(1, BLOCKS // 2 - 1) as b2:
                for a in range(2):
                    deg_block(b2 * 2 + a, a, False, False)
            deg_block(BLOCKS - 2, 0, False, False)
            deg_block(BLOCKS - 1, 1, False, True)
            pe.wait_ge(deg_ready, 1)
            for s in range(P // SUB):
                n = nc.tensor.matmul(ps_sub[:, s * HEAD:(s + 1) * HEAD], pick[:, s:s + 1], deg[:, 0:HEAD],
                                     start=True, stop=True)
            n.then_inc(sub_counted, 1)

            extra_turn = [pe.alloc_register(f"pe_extra{a}") for a in range(2)]
            for turn in extra_turn:
                pe.reg_mov(turn, 1)

            def joint_tile(to, sources, joint, k, first):
                for c in range(4):
                    m = nc.tensor.matmul(to[:, c, :], sources[:, :, k], joint[k][:, c * (JOINT // 4):(c + 1) * (JOINT // 4)],
                                         start=first, stop=True, skip_group_check=not first)
                return m

            def extra_tiles(to, a):
                pe.wait_ge(extra_ready[a], pe.snap(extra_turn[a]))
                for k in range(EXTRA):
                    m = joint_tile(to, src_extra[a], joint_extra[a], k, False)
                m.then_inc(extra_used[a], 1)
                pe.reg_add(extra_turn[a], extra_turn[a], 1)

            pe.wait_ge(sub_ready, 1)
            with pe.Fori(0, SUBS // 2) as s2:
                for a in range(2):
                    n = pe.value_load(sub_more[0:1, bass.ds(s2 * 2 + a, 1)], min_val=0, max_val=TILES // EXTRA)
                    pe.wait_ge(sub_copied, s2 * 2 + (a + 1))
                    pe.wait_ge(main_ready, s2 * 2 + (a + 1))
                    pe.sem_inc(pe_turn, 1)
                    for k in range(MAIN):
                        m = joint_tile(ps_count[a], src_main[a], joint_main[a], k, k == 0)
                    m.then_inc(main_used, 1)
                    with pe.If(n > 1):
                        with pe.Fori(0, n >> 1):
                            for b in range(2):
                                extra_tiles(ps_count[a], b)
                    with pe.If((n & 1) > 0):
                        extra_tiles(ps_count[a], 0)
                    nc.tensor.matmul(ps_count[a][:, 3, 0:1], zeros16[:, :], zeros16[:, 0:1],
                                     start=False, stop=True, skip_group_check=True).then_inc(built, 1)

            pe.wait_ge(mode_ready, 1)
            count = pe.alloc_register("pe_count")
            pe.reg_mov(count, 1)
            pair_next = pe.alloc_register("pe_pair")
            for p in range(PASSES):
                project(p, (w_gcn + [w_pre])[p][:, :])
                edge_pass(p)
                if p < GCN_LAYERS:
                    with pe.Fori(0, GROUPS // 2) as g2:
                        for h in range(2):
                            product_z(COLLECT(p), g2, h, both_halves[:, :])
            with pe.Fori(0, GROUPS // 2) as g2:
                for h in range(2):
                    product_z(POST, g2, h, w_post[:, :])


def kernel(x, src, dst, edge_attr_50, L0_gnn_W1, L0_gnn_b1, L0_gnn_W2, L0_gnn_b2, L0_gnn_W3, L0_gnn_b3,
           L1_gnn_W_pre, L1_gnn_b_pre, L1_gnn_W_rad, L1_gnn_b_rad, L1_gnn_W_post, L1_gnn_b_post):
    import concourse.bacc as bacc
    from concourse.bass_utils import run_bass_kernel_spmd

    def by_tile(a, fill):
        a = np.concatenate([np.asarray(a), np.full(BLOCKS * BLOCK - EDGES, fill, np.int32)])
        return np.ascontiguousarray(a.reshape(TILES, P).T)

    def row(b):
        return np.ascontiguousarray(np.asarray(b).reshape(1, -1))

    def turned(w):
        return np.ascontiguousarray(np.asarray(w).T)

    radial = np.zeros((RADIAL, BLOCKS * BLOCK), np.float32)
    radial[:, :EDGES] = np.asarray(edge_attr_50).T
    arrays = {
        "x": np.ascontiguousarray(x),
        "src": by_tile(src, 0),
        "dst": by_tile(dst, NODES),
        "radial": radial,
        "W1": np.ascontiguousarray(L0_gnn_W1), "b1": row(L0_gnn_b1),
        "W2": np.ascontiguousarray(L0_gnn_W2), "b2": row(L0_gnn_b2),
        "W3": np.ascontiguousarray(L0_gnn_W3), "b3": row(L0_gnn_b3),
        "W_pre": turned(L1_gnn_W_pre), "b_pre": row(L1_gnn_b_pre),
        "W_rad": turned(L1_gnn_W_rad), "b_rad": row(L1_gnn_b_rad),
        "W_post": turned(L1_gnn_W_post), "b_post": row(L1_gnn_b_post),
    }
    nc = bacc.Bacc("TRN2", target_bir_lowering=False, num_devices=1)
    args = {name: nc.dram_tensor(f"in_{name}", a.shape, mybir.dt.from_np(a.dtype), kind="ExternalInput").ap()
            for name, a in arrays.items()}
    out = nc.dram_tensor("out", (NODES, D), F32, kind="ExternalOutput").ap()
    gnn_program(nc, out=out, **args)
    result = run_bass_kernel_spmd(nc, [{f"in_{name}": a for name, a in arrays.items()}], core_ids=[0])
    return result.results[0]["out"]
```
